# Optimizing a Trainium2 kernel written in Bass

```python
import numpy as np
import jax
import jax.numpy as jnp

def _softmax(x, axis=-1):
    return jax.nn.softmax(x, axis=axis)

def _gelu(x):
    return jax.nn.gelu(x, approximate=True)

def _silu(x):
    return jax.nn.silu(x)

def _sigmoid(x):
    return jax.nn.sigmoid(x)

def _layernorm(x, axis=-1, eps=1e-05):
    m = jnp.mean(x, axis=axis, keepdims=True)
    v = jnp.var(x, axis=axis, keepdims=True)
    return (x - m) / jnp.sqrt(v + eps)

def _scatter_add(tgt, idx, src, axis=0):
    return tgt.at[idx].add(src)

def _segment_sum(src, seg, n):
    return jax.ops.segment_sum(src, seg, n)
kernel_name = 'mk_xattn_ffn_d1_seqx_r8_70bb96'

def setup_inputs(seed: int=0):
    np.random.seed(seed)
    _w = jnp.asarray

    def _rec_inputs():
        import jax
        import jax.numpy as jnp
        _rk = jax.random.key(seed)
        x = -0.000125 + 0.9999 * jax.random.normal(jax.random.fold_in(_rk, 1), (64, 128, 128), jnp.float32)
        _lenS = 128 - jax.random.randint(jax.random.fold_in(_rk, 7), (64,), 0, max(1, 128 // 4) + 1, jnp.int32)
        _lenS2 = 77 - jax.random.randint(jax.random.fold_in(_rk, 8), (64,), 0, max(1, 77 // 4) + 1, jnp.int32)
        _ctx_768P = jax.random.normal(jax.random.fold_in(_rk, 11), (64, 16, 96), jnp.float32)
        _ctx_768c = jax.random.dirichlet(jax.random.fold_in(_rk, 511), 0.3 * jnp.ones((16,), jnp.float32), (64, 77))
        _ctx_768t = jnp.einsum('bsk,bkd->bsd', _ctx_768c, _ctx_768P)
        _ctx_768t = _ctx_768t * jax.lax.rsqrt(jnp.mean(jnp.square(_ctx_768t)) + 1e-12) * 0.953939
        ctx_768 = 0.00272024 + 0.999456 * (_ctx_768t + 0.3 * jax.random.normal(jax.random.fold_in(_rk, 611), (64, 77, 96), jnp.float32))
        return (x, ctx_768)
    x, ctx_768 = _rec_inputs()

    def _L0_xattn_setup():
        import jax, jax.numpy as jnp
        import numpy as np
        N_HEADS = 16
        D_EMBED = 128
        D_CROSS = 96
        D_HEAD = D_EMBED // N_HEADS
        key = jax.random.key(seed)
        ks = jax.random.split(key, 10)
        B, SQ, SKV = (8, 512, 77)
        s_e = 1.0 / np.sqrt(D_EMBED)
        s_c = 1.0 / np.sqrt(D_CROSS)
        return {'x': jax.random.normal(ks[0], (B, SQ, D_EMBED), jnp.float32), 'y': jax.random.normal(ks[1], (B, SKV, D_CROSS), jnp.float32), 'wq': jax.random.normal(ks[2], (D_EMBED, D_EMBED), jnp.float32) * s_e, 'bq': jnp.zeros((D_EMBED,), jnp.float32), 'wk': jax.random.normal(ks[3], (D_CROSS, D_EMBED), jnp.float32) * s_c, 'bk': jnp.zeros((D_EMBED,), jnp.float32), 'wv': jax.random.normal(ks[4], (D_CROSS, D_EMBED), jnp.float32) * s_c, 'bv': jnp.zeros((D_EMBED,), jnp.float32), 'wo': jax.random.normal(ks[5], (D_EMBED, D_EMBED), jnp.float32) * s_e, 'bo': jnp.zeros((D_EMBED,), jnp.float32)}
    _L0_xattn_all = _L0_xattn_setup()
    _L0_xattn_in = {k: v for k, v in _L0_xattn_all.items() if k in ('wq', 'bq', 'wk', 'bk', 'wv', 'bv', 'wo', 'bo')}
    del _L0_xattn_all

    def _L0_ffn_setup():
        import jax, jax.numpy as jnp
        import numpy as np
        H = 128
        I = 88
        E = 64
        TOP_K = 8
        NG = 8
        TOPK_GROUP = 4
        N_SHARED = 2
        ROUTED_SCALE = 2.5
        S_I = I * N_SHARED

        def _route(x, gate_w, gate_bias):
            T = x.shape[0]
            logits = x @ gate_w.T
            scores = jax.nn.sigmoid(logits)
            scores_for_choice = scores + gate_bias[None, :]
            grp = scores_for_choice.reshape(T, NG, E // NG)
            group_scores = jnp.sum(jax.lax.top_k(grp, 2)[0], axis=-1)
            _, gidx = jax.lax.top_k(group_scores, TOPK_GROUP)
            gmask = jnp.zeros((T, NG), dtype=scores.dtype).at[jnp.arange(T)[:, None], gidx].set(1.0)
            emask = jnp.repeat(gmask, E // NG, axis=1)
            masked = jnp.where(emask > 0, scores_for_choice, 0.0)
            _, topk_idx = jax.lax.top_k(masked, TOP_K)
            topk_w = jnp.take_along_axis(scores, topk_idx, axis=1)
            topk_w = topk_w / (jnp.sum(topk_w, axis=-1, keepdims=True) + 1e-20)
            topk_w = topk_w * ROUTED_SCALE
            rw = jnp.zeros((T, E), dtype=scores.dtype).at[jnp.arange(T)[:, None], topk_idx].add(topk_w)
            return rw

        def _mlp(x, gw, uw, dw):
            return jax.nn.silu(x @ gw.T) * (x @ uw.T) @ dw.T
        key = jax.random.key(seed)
        ks = jax.random.split(key, 10)
        sc = 0.02
        return {'hidden_states': jax.random.normal(ks[0], (1, 128, H), dtype=jnp.float32), 'gate_w': sc * jax.random.normal(ks[1], (E, H), dtype=jnp.float32), 'gate_bias': sc * jax.random.normal(ks[2], (E,), dtype=jnp.float32), 'Wg': sc * jax.random.normal(ks[3], (E, I, H), dtype=jnp.float32), 'Wu': sc * jax.random.normal(ks[4], (E, I, H), dtype=jnp.float32), 'Wd': sc * jax.random.normal(ks[5], (E, H, I), dtype=jnp.float32), 'Sg': sc * jax.random.normal(ks[6], (S_I, H), dtype=jnp.float32), 'Su': sc * jax.random.normal(ks[7], (S_I, H), dtype=jnp.float32), 'Sd': sc * jax.random.normal(ks[8], (H, S_I), dtype=jnp.float32)}
    _L0_ffn_all = _L0_ffn_setup()
    _L0_ffn_in = {k: v for k, v in _L0_ffn_all.items() if k in ('gate_w', 'gate_bias', 'Wg', 'Wu', 'Wd', 'Sg', 'Su', 'Sd')}
    del _L0_ffn_all
    return {'x': x, 'ctx_768': ctx_768, 'L0_xattn_wq': _L0_xattn_in['wq'], 'L0_xattn_bq': _L0_xattn_in['bq'], 'L0_xattn_wk': _L0_xattn_in['wk'], 'L0_xattn_bk': _L0_xattn_in['bk'], 'L0_xattn_wv': _L0_xattn_in['wv'], 'L0_xattn_bv': _L0_xattn_in['bv'], 'L0_xattn_wo': _L0_xattn_in['wo'], 'L0_xattn_bo': _L0_xattn_in['bo'], 'L0_ffn_gate_w': _L0_ffn_in['gate_w'], 'L0_ffn_gate_bias': _L0_ffn_in['gate_bias'], 'L0_ffn_Wg': _L0_ffn_in['Wg'], 'L0_ffn_Wu': _L0_ffn_in['Wu'], 'L0_ffn_Wd': _L0_ffn_in['Wd'], 'L0_ffn_Sg': _L0_ffn_in['Sg'], 'L0_ffn_Su': _L0_ffn_in['Su'], 'L0_ffn_Sd': _L0_ffn_in['Sd']}

def reference(x, ctx_768, L0_xattn_wq, L0_xattn_bq, L0_xattn_wk, L0_xattn_bk, L0_xattn_wv, L0_xattn_bv, L0_xattn_wo, L0_xattn_bo, L0_ffn_gate_w, L0_ffn_gate_bias, L0_ffn_Wg, L0_ffn_Wu, L0_ffn_Wd, L0_ffn_Sg, L0_ffn_Su, L0_ffn_Sd):
    import jax
    import jax.numpy as jnp

    def _L0_xattn_ref(x, y, wq, bq, wk, bk, wv, bv, wo, bo):
        import jax, jax.numpy as jnp
        import numpy as np
        N_HEADS = 16
        D_EMBED = 128
        D_CROSS = 96
        D_HEAD = D_EMBED // N_HEADS
        B, SQ, _ = x.shape
        SKV = y.shape[1]
        q = (x @ wq + bq).reshape(B, SQ, N_HEADS, D_HEAD)
        k = (y @ wk + bk).reshape(B, SKV, N_HEADS, D_HEAD)
        v = (y @ wv + bv).reshape(B, SKV, N_HEADS, D_HEAD)
        scores = jnp.einsum('bqhd,bkhd->bhqk', q, k) / jnp.sqrt(jnp.asarray(D_HEAD, x.dtype))
        attn = jax.nn.softmax(scores, axis=-1)
        out = jnp.einsum('bhqk,bkhd->bqhd', attn, v).reshape(B, SQ, D_EMBED)
        return out @ wo + bo

    def _L0_ffn_ref(hidden_states, gate_w, gate_bias, Wg, Wu, Wd, Sg, Su, Sd):
        import jax, jax.numpy as jnp
        import numpy as np
        H = 128
        I = 88
        E = 64
        TOP_K = 8
        NG = 8
        TOPK_GROUP = 4
        N_SHARED = 2
        ROUTED_SCALE = 2.5
        S_I = I * N_SHARED

        def _route(x, gate_w, gate_bias):
            T = x.shape[0]
            logits = x @ gate_w.T
            scores = jax.nn.sigmoid(logits)
            scores_for_choice = scores + gate_bias[None, :]
            grp = scores_for_choice.reshape(T, NG, E // NG)
            group_scores = jnp.sum(jax.lax.top_k(grp, 2)[0], axis=-1)
            _, gidx = jax.lax.top_k(group_scores, TOPK_GROUP)
            gmask = jnp.zeros((T, NG), dtype=scores.dtype).at[jnp.arange(T)[:, None], gidx].set(1.0)
            emask = jnp.repeat(gmask, E // NG, axis=1)
            masked = jnp.where(emask > 0, scores_for_choice, 0.0)
            _, topk_idx = jax.lax.top_k(masked, TOP_K)
            topk_w = jnp.take_along_axis(scores, topk_idx, axis=1)
            topk_w = topk_w / (jnp.sum(topk_w, axis=-1, keepdims=True) + 1e-20)
            topk_w = topk_w * ROUTED_SCALE
            rw = jnp.zeros((T, E), dtype=scores.dtype).at[jnp.arange(T)[:, None], topk_idx].add(topk_w)
            return rw

        def _mlp(x, gw, uw, dw):
            return jax.nn.silu(x @ gw.T) * (x @ uw.T) @ dw.T
        B, S, _ = hidden_states.shape
        x = hidden_states.reshape(B * S, H)
        rw = _route(x, gate_w, gate_bias)
        expert_out = jax.vmap(lambda gw_, uw_, dw_: _mlp(x, gw_, uw_, dw_))(Wg, Wu, Wd)
        routed = jnp.einsum('eth,te->th', expert_out, rw)
        shared = _mlp(x, Sg, Su, Sd)
        out = (routed + shared).reshape(B, S, H)
        return out
    x = x + _L0_xattn_ref(_layernorm(x, axis=-1), ctx_768, L0_xattn_wq, L0_xattn_bq, L0_xattn_wk, L0_xattn_bk, L0_xattn_wv, L0_xattn_bv, L0_xattn_wo, L0_xattn_bo)
    x = x + _L0_ffn_ref(_layernorm(x, axis=-1), L0_ffn_gate_w, L0_ffn_gate_bias, L0_ffn_Wg, L0_ffn_Wu, L0_ffn_Wd, L0_ffn_Sg, L0_ffn_Su, L0_ffn_Sd)
    return x

_drawn_inputs = setup_inputs


def setup_inputs(seed=0):
    import zlib

    import numpy as np

    out = dict(_drawn_inputs(seed))
    spreads = {'L0_xattn_bq': (0.0, 0.325),
     'L0_xattn_bk': (0.0, 0.8),
     'L0_xattn_bv': (0.0, 0.1),
     'L0_xattn_bo': (0.0, 0.1)}
    factors = {'L0_ffn_gate_w': 8.0,
     'L0_ffn_gate_bias': 8.0,
     'L0_ffn_Wg': 8.0,
     'L0_ffn_Wu': 8.0,
     'L0_ffn_Wd': 8.0,
     'L0_ffn_Sg': 8.0,
     'L0_ffn_Su': 8.0,
     'L0_ffn_Sd': 8.0}
    for name, (base, spread) in spreads.items():
        noise = np.random.default_rng([zlib.crc32(name.encode()), seed]).standard_normal(out[name].shape)
        drawn = base * np.exp(spread * noise) if base else spread * noise
        out[name] = jnp.asarray(drawn.astype(out[name].dtype))
    for name, factor in factors.items():
        out[name] = (out[name] * factor).astype(out[name].dtype)
    return out
```

```python
from contextlib import ExitStack

import concourse.bass as bass
from concourse import mybir

F32 = mybir.dt.float32
BF16 = mybir.dt.bfloat16
I32 = mybir.dt.int32
ALU = mybir.AluOpType
ACT = mybir.ActivationFunctionType
X = mybir.AxisListType.X

P = 128
NT = 64
D = 128
DC = 96
SK = 77
NH, DH = 16, 8
QH = 4
G = 4
NG = NT // G
E, I = 64, 88
EG = 8
TOPG = 4
K = 8
ROUTED_SCALE = 2.5
EPS = 1e-5
GUESS = float(0x5F3759DF)
HALVES = 2
HG = NG // HALVES
HT = NT * P // HALVES
CAP = HT + P
BT = HT * K // P + E
DUMMY = BT - HT * K // P
XROWS = E * CAP + DUMMY * P
RW = D + K + 1
TOKENS = NT * P
BG = BT // G
STEPS = HALVES * BG // NG
RING = 5
TC = BT // E
WG1 = I + 1
WGU = 2 * I + 1
FAR = 1.0e6
TAKEN = -3.0e38


def moe_block(nc, x, ctxt, wq, bq, wk, bk, wv, bv, wo, bo, gatet, gbias, wgt, wut, wdt, sgt, sut, sdt, out):
    ctx = ExitStack()
    with ctx:
        def sb(name, shape, dt=F32):
            return ctx.enter_context(nc.sbuf_tensor(name, shape, dt))

        def sem(name):
            return ctx.enter_context(nc.semaphore(name))

        routed_rows = [nc.dram_tensor(f"routed_rows{h}", [XROWS, RW], F32, kind="Internal").ap()
                       for h in range(HALVES)]
        normed_t = nc.dram_tensor("normed_t", [NG * P, G * P], F32, kind="Internal").ap()
        expert_out = nc.dram_tensor("expert_out", [TOKENS * K, D], F32, kind="Internal").ap()

        wq_sb = sb("wq_sb", [P, D])
        bq_sb = sb("bq_sb", [P, 1])
        wk_sb = sb("wk_sb", [DC + 1, D])
        wv_sb = sb("wv_sb", [DC + 1, D])
        wo_sb = sb("wo_sb", [P, D])
        bo_sb = sb("bo_sb", [1, D])
        gate_sb = sb("gate_sb", [P, E])
        gbias_sb = sb("gbias_sb", [P, E])
        wgu = sb("wgu", [P, E, WGU])
        wd = sb("wd", [I, E, D])
        sg_w = sb("sg_w", [P, 2 * I])
        su_w = sb("su_w", [P, 2 * I])
        sd_w = sb("sd_w", [I, 2, D])
        ident = sb("ident", [P, P])
        upper = sb("upper", [P, P], BF16)
        ones_bf = sb("ones_bf", [P, P], BF16)
        ones_row = sb("ones_row", [1, P])
        head_bd = sb("head_bd", [P, NH])
        head_mask = sb("head_mask", [P, QH])
        before = sb("before", [P, EG, EG])
        key_start = sb("key_start", [P, E])
        tok8 = sb("tok8", [P, NT])
        rank8 = sb("rank8", [P, K])
        part1 = sb("part1", [P, 1])
        tile_no = sb("tile_no", [E, TC])
        pad_rows = sb("pad_rows", [P, RW])
        ones_e = sb("ones_e", [P, E])

        xres = sb("xres", [P, NT * D])
        score_sum = sb("score_sum", [P, NT])
        out_scale = sb("out_scale", [P, NT])
        own_key = sb("own_key", [P, HALVES * BT])
        tile_row = sb("tile_row", [1, HALVES * BT], I32)
        tile_exp = sb("tile_exp", [1, HALVES * BT], I32)
        pad_row = sb("pad_row", [1, HALVES * E], I32)

        SCW = NH * SK
        arena = sb("arena", [P, 8200])
        at = [0]

        def carve(width):
            a = arena[:, at[0]:at[0] + width]
            at[0] += width
            assert at[0] <= 8200
            return a

        q_t = [carve(G * P) for _ in range(2)]
        k_bd = [carve(G * QH * SK) for _ in range(2)]
        shifted = carve(SCW)
        probs = carve(SCW)
        probs_t = carve(NH * P)
        at[0] = 0
        rin_f = [carve(G * RW) for _ in range(RING)]
        rin = [r.rearrange("p (u w) -> p u w", w=RW) for r in rin_f]
        ring_y = [carve(G * D).rearrange("p (u d) -> p u d", d=D) for _ in range(RING)]
        b_xt = carve(G * P)
        b_sig = [carve(G * WG1).rearrange("p (b u w) -> p b u w", b=2, u=2) for _ in range(2)]
        b_h = carve(G * I)
        b_ht = carve(G * P)

        ctx_sb = [sb(f"ctx_sb{i}", [DC + 1, G * SK]) for i in range(2)]
        v_aug = [sb(f"v_aug{i}", [SK, G * NH * (DH + 1)]) for i in range(2)]
        xn = sb("xn", [P, G * D])
        xn_t = sb("xn_t", [P, G * P])
        stats = sb("stats", [P, G, 6])
        mv = sb("mv", [P, G, 2])
        rstd = sb("rstd", [P, G])
        stats2 = sb("stats2", [P, G, 6])
        mv2 = sb("mv2", [P, G, 2])
        rstd2 = sb("rstd2", [P, G])
        var_eps = sb("var_eps", [P, G])
        var_half = sb("var_half", [P, G])
        guess = sb("guess", [P, G], I32)
        square = sb("square", [P, G])
        row_max = sb("row_max", [P, 2, 2, QH])
        rden = sb("rden", [P, NH])
        ao = sb("ao", [P, D])
        ao_t = sb("ao_t", [P, P])
        rows = [sb(f"rows{i}", [P, G, RW]) for i in range(2)]
        slots = [sb(f"slots{i}", [P, G, K], I32) for i in range(2)]
        xn2_t = [sb(f"xn2_t{i}", [P, G * P]) for i in range(2)]
        es = sb("es", [P, G, E])
        score = sb("score", [P, G, E])
        choice = sb("choice", [P, G, E])
        masked = sb("masked", [P, G, E])
        taken = sb("taken", [P, G, E])
        tmp = sb("tmp", [P, G, E])
        tmp2 = sb("tmp2", [P, G, E])
        hi4 = sb("hi4", [P, G * EG, 4])
        lo4 = sb("lo4", [P, G * EG, 4])
        hi2 = sb("hi2", [P, G * EG, 2])
        lo2 = sb("lo2", [P, G * EG, 2])
        mid2 = sb("mid2", [P, G * EG, 2])
        hi1 = sb("hi1", [P, G * EG])
        lo1 = sb("lo1", [P, G * EG])
        mid1 = sb("mid1", [P, G * EG])
        gscore = sb("gscore", [P, G, EG])
        gmask = sb("gmask", [P, G, EG])
        top8 = sb("top8", [P, G, K])
        chosen = sb("chosen", [P, G, E], BF16)
        base = sb("base", [P, E])
        cnt_i = sb("cnt_i", [P, E], I32)
        n_tiles = sb("n_tiles", [P, E])
        tiles_end = sb("tiles_end", [P, E])
        cmp = sb("cmp", [E, TC, E])
        cmp2 = sb("cmp2", [E, TC, E])
        t_exp = sb("t_exp", [E, TC])
        t_cst = sb("t_cst", [E, TC])
        t_row = sb("t_row", [E, TC])
        idx_ring = [sb(f"idx_ring{r}", [P, G], I32) for r in range(RING)]
        key_eq = sb("key_eq", [P, G, K])
        key_rk = sb("key_rk", [P, G])

        banks = ctx.enter_context(nc.psum_tensor("banks", [P, 8, 512], F32))
        T = [banks[:, 4, :], banks[:, 5, :]]
        M0 = banks[:, 6, :]
        M1 = banks[:, 7, :]
        PX, PH, PY = banks[:, 4, :], banks[:, 5, :], banks[:, 2, :]
        PG = banks[:, 0:2, 0:2 * WGU].rearrange("p b (u w) -> p b u w", w=WGU)
        SHG, SHU, SHO = banks[:, 3, :], banks[:, 6, :], banks[:, 7, :]
        sh_x = sb("sh_x", [P, G * P])
        sh_sig = sb("sh_sig", [I, G * P])
        sh_h = sb("sh_h", [I, 2, G * P])

        c_ring = [wgu[:, :, :].rearrange("p e w -> p (e w)")[:, r * K * D:(r + 1) * K * D] for r in range(G)]

        s_x = sem("s_x")
        s_xrest = sem("s_xrest")
        s_w = sem("s_w")
        s_wexp = sem("s_wexp")
        s_ctx = [sem(f"s_ctx{i}") for i in range(2)]
        s_scat = [sem(f"s_scat{i}") for i in range(2)]
        s_pad = sem("s_pad")
        s_norm = [sem(f"s_norm{i}") for i in range(2)]
        s_shx = sem("s_shx")
        s_rin = [sem(f"s_rin{r}") for r in range(RING)]
        s_ysc = [sem(f"s_ysc{r}") for r in range(RING)]
        s_cin = [sem(f"s_cin{r}") for r in range(G)]
        s_out = sem("s_out")
        g_turn = sem("g_turn")
        s_const = sem("s_const")
        s_init = sem("s_init")
        s_vinit = sem("s_vinit")
        p_tr1 = sem("p_tr1")
        p_q = sem("p_q")
        p_k = sem("p_k")
        p_v = sem("p_v")
        p_sc = sem("p_sc")
        p_pt = sem("p_pt")
        p_pv = sem("p_pv")
        p_aot = sem("p_aot")
        p_proj = sem("p_proj")
        p_tr2 = sem("p_tr2")
        p_logit = sem("p_logit")
        p_rank = sem("p_rank")
        p_tab = sem("p_tab")
        p_bx = sem("p_bx")
        p_bgu = sem("p_bgu")
        p_bht = sem("p_bht")
        p_by = sem("p_by")
        p_shgu = sem("p_shgu")
        p_sho = sem("p_sho")
        a_xnt = sem("a_xnt")
        a_q = sem("a_q")
        a_v = sem("a_v")
        a_exp = sem("a_exp")
        a_pt = sem("a_pt")
        a_aot = sem("a_aot")
        a_xn2t = sem("a_xn2t")
        a_es = sem("a_es")
        a_bx = sem("a_bx")
        a_bht = sem("a_bht")
        a_bsig = sem("a_bsig")
        a_shsig = sem("a_shsig")
        d_xn = sem("d_xn")
        d_bd = sem("d_bd")
        d_sub = sem("d_sub")
        d_ao = sem("d_ao")
        d_res = sem("d_res")
        d_xn2 = sem("d_xn2")
        d_chosen = sem("d_chosen")
        d_slots = sem("d_slots")
        d_tab = sem("d_tab")
        d_tabe = sem("d_tabe")
        d_bh = sem("d_bh")
        d_by = sem("d_by")
        d_shh = sem("d_shh")
        d_sho = sem("d_sho")
        d_fin = sem("d_fin")

        def wait(eng, s, value):
            if not (isinstance(value, int) and value <= 0):
                eng.wait_ge(s, value)

        def scores_view(h):
            return banks[:, 2 * h:2 * h + 2, 0:QH * SK].rearrange("p b (j k) -> p b j k", k=SK)

        def half_view(t, h):
            return t[:, h * SCW // 2:(h + 1) * SCW // 2].rearrange("p (b j k) -> p b j k", b=2, k=SK)

        block = ctx.enter_context(nc.Block())

        @block.sync
        def _(sp):
            x_v = x.rearrange("t p d -> p t d")
            xres_v = xres[:, :].rearrange("p (t d) -> p t d", d=D)
            sp.dma_start(xres_v[:, 0:G, :], x_v[:, 0:G, :]).then_inc(s_x, 16)
            sp.dma_start(wq_sb[:, :], wq).then_inc(s_w, 16)
            sp.dma_start(bq_sb[:, :], bq.rearrange("(p a) -> p a", a=1)).then_inc(s_w, 16)

            def load_ctx(i2, p):
                g = 2 * i2 + p
                wait(sp, p_v, g - 1)
                sp.dma_start(ctx_sb[p][0:DC, :], ctxt[:, bass.ds(g * (G * SK), G * SK)]).then_inc(s_ctx[p], 16)

            load_ctx(0, 0)
            load_ctx(0, 1)
            sp.dma_start(xres_v[:, G:NT, :], x_v[:, G:NT, :]).then_inc(s_xrest, 16)
            sp.dma_start(wgu[:, :, 0:I], wgt).then_inc(s_wexp, 16)
            sp.dma_start(wgu[:, :, WG1:WGU], wut).then_inc(s_wexp, 16)
            sp.dma_start(wd[:, :, :], wdt).then_inc(s_wexp, 16)
            sp.wait_ge(s_init, 1)
            for h in range(HALVES):
                sp.dma_start(routed_rows[h][E * CAP:XROWS, :].rearrange("(r p) w -> p r w", p=P),
                             pad_rows[:, :].rearrange("p (a w) -> p a w", a=1).to_broadcast([P, DUMMY, RW])
                             ).then_inc(s_pad, 16)

            def pads(h):
                sp.wait_ge(d_tabe, 2 * h + 2)
                with sp.Fori(0, E // G) as i:
                    for u in range(G):
                        r = sp.value_load(pad_row[0:1, bass.ds(i * G + (h * E + u), 1)], min_val=0,
                                          max_val=E * CAP - P)
                        sp.dma_start(routed_rows[h][bass.ds(r, P), :], pad_rows[:, :]).then_inc(s_pad, 16)

            with sp.Fori(1, HG // 2 + 1) as i2:
                load_ctx(i2, 0)
                load_ctx(i2, 1)
            pads(0)
            with sp.Fori(HG // 2 + 1, NG // 2) as i2:
                load_ctx(i2, 0)
                load_ctx(i2, 1)

            def load_shared(i):
                wait(sp, p_shgu, 2 * i)
                sp.dma_start(sh_x[:, :], normed_t[bass.ds(i * P, P), :]).then_inc(s_shx, 16)

            def load_rows(h, i, q):
                j = STEPS * i + q
                r = q % RING
                if not (isinstance(i, int) and j < RING):
                    sp.wait_ge(d_by, j - (RING - 1))
                    sp.wait_ge(p_bx, j - (RING - 1))
                for u in range(G):
                    row = sp.value_load(tile_row[0:1, bass.ds(j * G + u, 1)], min_val=0, max_val=XROWS - P)
                    sp.dma_start(rin[r][:, u, :], routed_rows[h][bass.ds(row, P), :]).then_inc(s_rin[r], 16)

            sp.wait_ge(d_slots, HG + 2)
            sp.wait_ge(s_pad, 16 * (HALVES + E))
            sp.wait_ge(d_res, NT)
            for p in range(2):
                sp.wait_ge(s_norm[p], 16 * NG // 2)
            load_shared(0)
            for q in range(STEPS):
                load_rows(0, 0, q)
            with sp.Fori(1, NG // 2) as i:
                load_shared(i)
                for q in range(STEPS):
                    load_rows(0, i, q)
            pads(1)
            for p in range(2):
                sp.wait_ge(s_scat[p], 16 * G * K * NG // 2)
            sp.wait_ge(s_pad, 16 * (HALVES + 2 * E))
            with sp.Fori(NG // 2, NG) as i:
                load_shared(i)
                for q in range(STEPS):
                    load_rows(1, i, q)

            for r in range(RING):
                sp.wait_ge(s_ysc[r], 16 * G * HALVES * BG // RING)
            back = expert_out.rearrange("(n k) d -> n (k d)", k=K)

            def load_back(i, r):
                if not isinstance(i, int):
                    sp.wait_ge(d_fin, i * G + (r + 1 - G))
                sp.dma_start(c_ring[r], back[bass.ds((i * G + r) * P, P), :]).then_inc(s_cin[r], 16)

            for r in range(G):
                load_back(0, r)
            with sp.Fori(1, NG) as i:
                for r in range(G):
                    load_back(i, r)
            sp.wait_ge(s_out, 16 * NG)

        @block.gpsimd
        def _(pool):
            nc.gpsimd.memset(ident[:, :], 0.0).then_inc(s_const, 1)
            nc.gpsimd.memset(upper[:, :], 1.0).then_inc(s_const, 1)
            nc.gpsimd.memset(head_bd[:, :], 1.0).then_inc(s_const, 1)
            nc.gpsimd.memset(before[:, :, :], 1.0).then_inc(s_const, 1)
            pool.wait_ge(s_const, 4)
            nc.gpsimd.affine_select(out=ident[:, :], in_=ident[:, :], compare_op=ALU.not_equal, fill=1.0,
                                    base=0, pattern=[[-1, P]], channel_multiplier=1).then_inc(s_const, 1)
            nc.gpsimd.affine_select(out=upper[:, :], in_=upper[:, :], compare_op=ALU.is_gt, fill=0.0,
                                    base=0, pattern=[[1, P]], channel_multiplier=-1).then_inc(s_const, 1)
            nc.gpsimd.affine_select(out=head_bd[:, :], in_=head_bd[:, :], compare_op=ALU.is_ge, fill=0.0,
                                    base=0, pattern=[[-DH, NH]], channel_multiplier=1).then_inc(s_const, 1)
            nc.gpsimd.affine_select(out=before[:, :, :], in_=before[:, :, :], compare_op=ALU.is_gt, fill=0.0,
                                    base=0, pattern=[[1, EG], [-1, EG]], channel_multiplier=0).then_inc(s_const, 1)
            pool.wait_ge(s_const, 8)
            nc.gpsimd.affine_select(out=head_bd[:, :], in_=head_bd[:, :], compare_op=ALU.is_ge, fill=0.0,
                                    base=DH - 1, pattern=[[DH, NH]], channel_multiplier=-1).then_inc(s_const, 1)
            imprecise = dict(allow_small_or_imprecise_dtypes=True)
            nc.gpsimd.iota(key_start[:, :], [[CAP, E]], base=1, channel_multiplier=0, **imprecise)
            nc.gpsimd.iota(tok8[:, :], [[P * K, NT]], base=0, channel_multiplier=K, **imprecise)
            nc.gpsimd.iota(rank8[:, :], [[1, K]], base=0, channel_multiplier=0, **imprecise)
            nc.gpsimd.iota(part1[:, :], [[0, 1]], base=1, channel_multiplier=1, **imprecise)
            nc.gpsimd.iota(tile_no[:, :], [[E, TC]], base=0, channel_multiplier=1, **imprecise).then_inc(s_const, 1)

            def scatter(h, i2, p):
                pool.wait_ge(d_slots, 2 * i2 + (p + 1))
                pool.sem_inc(g_turn, 1)
                for u in range(G):
                    for k in range(K):
                        nc.gpsimd.indirect_dma_start(
                            out=routed_rows[h], out_offset=bass.IndirectOffsetOnAxis(ap=slots[p][:, u, k:k + 1], axis=0),
                            in_=rows[p][:, u, :], in_offset=None).then_inc(s_scat[p], 16)

            for h in range(HALVES):
                with pool.Fori(h * HG // 2, (h + 1) * HG // 2) as i2:
                    scatter(h, i2, 0)
                    scatter(h, i2, 1)
            with pool.Fori(0, NG) as i:
                for q in range(STEPS):
                    r = q % RING
                    pool.wait_ge(d_by, STEPS * i + (q + 1))
                    pool.sem_inc(g_turn, 1)
                    for u in range(G):
                        nc.gpsimd.indirect_dma_start(
                            out=expert_out, out_offset=bass.IndirectOffsetOnAxis(ap=idx_ring[r][:, u:u + 1], axis=0),
                            in_=ring_y[r][:, u, :], in_offset=None, bounds_check=TOKENS * K - 1,
                            oob_is_err=False).then_inc(s_ysc[r], 16)

        @block.scalar
        def _(act):
            act.dma_start(wk_sb[0:DC, :], wk).then_inc(s_w, 16)
            act.dma_start(wk_sb[DC:DC + 1, :], bk.rearrange("(a n) -> a n", a=1)).then_inc(s_w, 16)
            act.dma_start(wv_sb[0:DC, :], wv).then_inc(s_w, 16)
            act.dma_start(wv_sb[DC:DC + 1, :], bv.rearrange("(a n) -> a n", a=1)).then_inc(s_w, 16)
            act.dma_start(wo_sb[:, :], wo).then_inc(s_w, 16)
            act.dma_start(bo_sb[:, :], bo.rearrange("(a n) -> a n", a=1)).then_inc(s_w, 16)
            act.dma_start(gate_sb[:, :], gatet).then_inc(s_w, 16)
            act.dma_start(gbias_sb[:, :], gbias.rearrange("(a n) -> a n", a=1).to_broadcast([P, E])).then_inc(s_w, 16)
            act.dma_start(sg_w[:, :], sgt).then_inc(s_wexp, 16)
            act.dma_start(su_w[:, :], sut).then_inc(s_wexp, 16)
            act.dma_start(sd_w[:, :, :], sdt.rearrange("(a i) d -> i a d", i=I)).then_inc(s_wexp, 16)

            def prep_q(gp, p):
                act.wait_ge(p_tr1, gp + 1)
                nc.scalar.activation(xn_t[:, :], M0, ACT.Copy).then_inc(a_xnt, 1)
                act.wait_ge(p_q, gp + 1)
                nc.scalar.activation(q_t[p], M0, ACT.Identity, bias=bq_sb[:, 0:1]).then_inc(a_q, 1)

            def prep_v(gp, p):
                act.wait_ge(p_v, gp + 1)
                if isinstance(gp, int) and gp < 2:
                    act.wait_ge(s_vinit, 1)
                dst = v_aug[p][:, :].rearrange("k (n c) -> k n c", c=DH + 1)[:, :, 0:DH]
                nc.scalar.activation(dst, M0[0:SK, :].rearrange("k (n c) -> k n c", c=DH), ACT.Copy).then_inc(a_v, 1)

            def rest(t):
                for i in range(4):
                    act.wait_ge(p_pt, 4 * t + (i + 1))
                    nc.scalar.activation(probs_t[0:SK, i * 512:(i + 1) * 512], T[i % 2][0:SK, :],
                                         ACT.Copy).then_inc(a_pt, 1)

            def exp(t, h):
                act.wait_ge(d_sub, 2 * t + (h + 1))
                nc.scalar.activation(probs[:, h * SCW // 2:(h + 1) * SCW // 2],
                                     shifted[:, h * SCW // 2:(h + 1) * SCW // 2], ACT.Exp,
                                     scale=float(DH) ** -0.5).then_inc(a_exp, 1)

            def attn_t(t):
                act.wait_ge(p_aot, t + 1)
                nc.scalar.activation(ao_t[:, :], M1[:, 0:P], ACT.Copy).then_inc(a_aot, 1)

            def route(g, i2, p):
                act.wait_ge(p_tr2, g + 1)
                wait(act, s_norm[p], 16 * i2)
                nc.scalar.activation(xn2_t[p][:, :], M0, ACT.Copy).then_inc(a_xn2t, 1)
                act.wait_ge(p_logit, g + 1)
                nc.scalar.activation(es[:, :, :], M0[:, 0:G * E].rearrange("p (u e) -> p u e", e=E), ACT.Exp,
                                     scale=-1.0).then_inc(a_es, 1)
                act.wait_ge(a_xn2t, g + 1)
                act.dma_start(normed_t[bass.ds(g * P, P), :], xn2_t[p][:, :]).then_inc(s_norm[p], 16)

            def step(i2, p, first=False, last=False):
                g = 2 * i2 + p
                for u in range(G):
                    t = G * g + u
                    if not (first and u == 0):
                        rest(t - 1)
                    exp(t, 0)
                    if not (first and u == 0):
                        attn_t(t - 1)
                    exp(t, 1)
                    if u == 0 and not last:
                        prep_q(g + 1, 1 - p)
                    if u == 1 and not last:
                        prep_v(g + 1, 1 - p)
                    if u == 1 and not first:
                        route(g - 1, i2 - 1 + p, 1 - p)

            prep_q(0, 0)
            prep_v(0, 0)
            step(0, 0, first=True)
            step(0, 1)
            with act.Fori(1, NG // 2 - 1) as i2:
                step(i2, 0)
                step(i2, 1)
            step(NG // 2 - 1, 0)
            step(NG // 2 - 1, 1, last=True)
            rest(NT - 1)
            attn_t(NT - 1)
            route(NG - 1, NG // 2 - 1, 1)

            def front(j, p):
                act.wait_ge(p_bx, j + 1)
                nc.scalar.activation(b_xt, PX, ACT.Copy).then_inc(a_bx, 1)
                act.wait_ge(p_bgu, j + 1)
                nc.scalar.activation(b_sig[p], PG[:, :, :, 0:WG1], ACT.Sigmoid).then_inc(a_bsig, 1)

            def expert_steps(i, last=False):
                for q in range(STEPS):
                    j = STEPS * i + q
                    more = not (last and q == STEPS - 1)
                    if more:
                        act.wait_ge(p_bx, j + 2)
                        nc.scalar.activation(b_xt, PX, ACT.Copy).then_inc(a_bx, 1)
                    act.wait_ge(p_bht, j + 1)
                    nc.scalar.activation(b_ht[0:I, :], PH[0:I, :], ACT.Copy).then_inc(a_bht, 1)
                    if more:
                        act.wait_ge(p_bgu, j + 2)
                        nc.scalar.activation(b_sig[(q + 1) % 2], PG[:, :, :, 0:WG1], ACT.Sigmoid).then_inc(a_bsig, 1)
                    if q in (3, 6):
                        a = (q - 3) // 3
                        act.wait_ge(p_shgu, 2 * i + (a + 1))
                        nc.scalar.activation(sh_sig[:, :], SHG[0:I, :], ACT.Sigmoid).then_inc(a_shsig, 1)

            front(0, 0)
            with act.Fori(0, NG - 1) as i:
                expert_steps(i)
            expert_steps(NG - 1, last=True)

            def store(i):
                act.wait_ge(d_fin, G * i + G)
                act.dma_start(out[bass.ds(i * G, G), :, :].rearrange("t p d -> p t d"),
                              xres[:, bass.ds(i * (G * D), G * D)].rearrange("p (t d) -> p t d", d=D)
                              ).then_inc(s_out, 16)

            with act.Fori(0, NG) as i:
                store(i)
            act.wait_ge(s_out, 16 * NG)

        @block.vector
        def _(dve):
            v = nc.vector

            def drain():
                dve.drain()

            def norm(src_group, dst, st, m, r, ready):
                for u in range(G):
                    v.bn_stats(st[:, u, :], xres[:, bass.ds(src_group * (G * D) + u * D, D)])
                drain()
                for u in range(G):
                    v.bn_aggr(m[:, u, :], st[:, u, :])
                drain()
                v.tensor_scalar(var_eps[:, :], m[:, :, 1], EPS, None, ALU.add)
                v.tensor_scalar(var_half[:, :], m[:, :, 1], -0.5, -0.5 * EPS, ALU.mult, ALU.add)
                drain()
                v.tensor_scalar(guess[:, :], var_eps[:, :].bitcast(I32), 1, None, ALU.arith_shift_right)
                drain()
                v.tensor_scalar(r[:, :].bitcast(I32), guess[:, :], -1.0, GUESS, ALU.mult, ALU.add)
                drain()
                for _ in range(3):
                    v.tensor_tensor(square[:, :], r[:, :], r[:, :], ALU.mult)
                    drain()
                    v.tensor_tensor(square[:, :], square[:, :], var_half[:, :], ALU.mult)
                    drain()
                    v.scalar_tensor_tensor(out=r[:, :], in0=square[:, :], scalar=1.5, in1=r[:, :],
                                           op0=ALU.add, op1=ALU.mult)
                    drain()
                for u in range(G):
                    last = v.tensor_scalar(dst(u), xres[:, bass.ds(src_group * (G * D) + u * D, D)],
                                           m[:, u, 0:1], r[:, u:u + 1], ALU.subtract, ALU.mult)
                last.then_inc(ready, 1)

            def prep_norm(gp):
                wait(dve, p_tr1, gp)
                norm(gp, lambda u: xn[:, u * D:(u + 1) * D], stats, mv, rstd, d_xn)

            def prep_keys(gp, p):
                dve.wait_ge(p_k, gp + 1)
                v.tensor_tensor(
                    k_bd[p].rearrange("p (u j k) -> p u j k", u=G, j=QH),
                    M0[:, 0:G * SK].rearrange("p (u a k) -> p u a k", u=G, a=1).to_broadcast([P, G, QH, SK]),
                    head_mask[:, :].rearrange("p (a j b) -> p a j b", a=1, b=1).to_broadcast([P, G, QH, SK]),
                    ALU.mult).then_inc(d_bd, 1)

            def shift(t, h):
                dve.wait_ge(p_sc, 2 * t + (h + 1))
                v.tensor_reduce(row_max[:, h, :, :], scores_view(h), X, ALU.max)
                drain()
                wait(dve, a_exp, 2 * t + (h - 1))
                v.tensor_tensor(half_view(shifted, h), scores_view(h),
                                row_max[:, h, :, :].rearrange("p b (j a) -> p b j a", a=1).to_broadcast([P, 2, QH, SK]),
                                ALU.subtract).then_inc(d_sub, 1)

            def attn_norm(t):
                dve.wait_ge(p_pv, t + 1)
                pv = M1[:, 0:NH * (DH + 1)].rearrange("p (n c) -> p n c", c=DH + 1)
                v.reciprocal(rden[:, :], pv[:, :, DH])
                drain()
                v.tensor_tensor(ao[:, :].rearrange("p (n c) -> p n c", c=DH), pv[:, :, 0:DH],
                                rden[:, :].rearrange("p (n a) -> p n a", a=1).to_broadcast([P, NH, DH]),
                                ALU.mult).then_inc(d_ao, 1)

            def residual(t):
                dve.wait_ge(p_proj, t + 1)
                xt = xres[:, bass.ds(t * D, D)]
                v.tensor_tensor(xt, M1[:, P:2 * P], xt, ALU.add).then_inc(d_res, 1)

            def route_norm(g, i2, p):
                wait(dve, s_scat[p], 16 * G * K * i2)
                norm(g, lambda u: rows[p][:, u, 0:D], stats2, mv2, rstd2, d_xn2)
                v.tensor_copy(rows[p][:, :, D + K], tok8[:, bass.ds(g * G, G)])

            def route_groups(g):
                dve.wait_ge(a_es, g + 1)
                v.tensor_scalar(tmp[:, :, :], es[:, :, :], 1.0, None, ALU.add)
                drain()
                v.reciprocal(score[:, :, :], tmp[:, :, :])
                drain()
                v.tensor_tensor(choice[:, :, :], score[:, :, :],
                                gbias_sb[:, :].rearrange("p (a e) -> p a e", a=1).to_broadcast([P, G, E]), ALU.add)
                drain()
                cg = choice[:, :, :].rearrange("p u (g k) -> p (u g) k", k=EG)
                v.tensor_tensor(hi4[:, :, :], cg[:, :, 0:4], cg[:, :, 4:8], ALU.max)
                v.tensor_tensor(lo4[:, :, :], cg[:, :, 0:4], cg[:, :, 4:8], ALU.min)
                drain()
                v.tensor_tensor(hi2[:, :, :], hi4[:, :, 0:2], hi4[:, :, 2:4], ALU.max)
                v.tensor_tensor(mid2[:, :, :], hi4[:, :, 0:2], hi4[:, :, 2:4], ALU.min)
                v.tensor_tensor(lo2[:, :, :], lo4[:, :, 0:2], lo4[:, :, 2:4], ALU.max)
                drain()
                v.tensor_tensor(lo2[:, :, :], lo2[:, :, :], mid2[:, :, :], ALU.max)
                v.tensor_tensor(hi1[:, :], hi2[:, :, 0], hi2[:, :, 1], ALU.max)
                v.tensor_tensor(mid1[:, :], hi2[:, :, 0], hi2[:, :, 1], ALU.min)
                drain()
                v.tensor_tensor(lo1[:, :], lo2[:, :, 0], lo2[:, :, 1], ALU.max)
                drain()
                v.tensor_tensor(lo1[:, :], lo1[:, :], mid1[:, :], ALU.max)
                drain()
                v.tensor_tensor(gscore[:, :, :].rearrange("p u g -> p (u g)"), hi1[:, :], lo1[:, :], ALU.add)
                drain()
                gi = gscore[:, :, :].rearrange("p u (i a) -> p u i a", a=1).to_broadcast([P, G, EG, EG])
                gj = gscore[:, :, :].rearrange("p u (a j) -> p u a j", a=1).to_broadcast([P, G, EG, EG])
                t4 = tmp[:, :, :].rearrange("p u (i j) -> p u i j", j=EG)
                u4 = tmp2[:, :, :].rearrange("p u (i j) -> p u i j", j=EG)
                v.tensor_tensor(t4, gj, gi, ALU.is_gt)
                v.tensor_tensor(u4, gj, gi, ALU.is_equal)
                drain()
                bef = before[:, :, :].rearrange("p i (a j) -> p a i j", a=1).to_broadcast([P, G, EG, EG])
                v.tensor_tensor(u4, u4, bef, ALU.mult)
                drain()
                v.tensor_tensor(t4, t4, u4, ALU.add)
                drain()
                v.tensor_reduce(gmask[:, :, :], t4, X, ALU.add)
                drain()
                v.tensor_scalar(gmask[:, :, :], gmask[:, :, :], float(TOPG), None, ALU.is_lt)
                drain()
                v.tensor_tensor(masked[:, :, :].rearrange("p u (g k) -> p (u g) k", k=EG), cg,
                                gmask[:, :, :].rearrange("p u (g a) -> p (u g) a", a=1).to_broadcast([P, G * EG, EG]),
                                ALU.mult)
                drain()

            def route_top(g):
                for u in range(G):
                    v.max(top8[:, u, :], masked[:, u, :])
                drain()
                for u in range(G):
                    v.match_replace(out=taken[:, u, :], in_to_replace=top8[:, u, :], in_values=masked[:, u, :],
                                    imm_value=TAKEN)
                drain()
                v.tensor_scalar(chosen[:, :, :], taken[:, :, :], TAKEN / 2, None, ALU.is_lt).then_inc(d_chosen, 1)
                drain()
                v.tensor_tensor(tmp[:, :, :], score[:, :, :], chosen[:, :, :], ALU.mult)
                drain()
                v.tensor_reduce(score_sum[:, bass.ds(g * G, G)], tmp[:, :, :], X, ALU.add)

            def route_slots(g, p):
                dve.wait_ge(p_rank, g + 1)
                rk = M0[:, 0:G * E].rearrange("p (u e) -> p u e", e=E)
                v.tensor_tensor(tmp2[:, :, :], rk,
                                base[:, :].rearrange("p (a e) -> p a e", a=1).to_broadcast([P, G, E]), ALU.add)
                drain()
                v.tensor_tensor(base[:, :], M0[:, G * E:G * E + E], base[:, :], ALU.add)
                v.tensor_tensor(tmp2[:, :, :], tmp2[:, :, :], chosen[:, :, :], ALU.mult)
                drain()
                for u in range(G):
                    v.max(rows[p][:, u, D:D + K], tmp2[:, u, :])
                drain()
                v.tensor_scalar(slots[p][:, :, :], rows[p][:, :, D:D + K], -1.0, None,
                                ALU.add).then_inc(d_slots, 1)

            def table(h):
                v.tensor_scalar(pad_row[0:1, h * E:(h + 1) * E], base[0:1, :], -1.0, None, ALU.add)
                v.tensor_tensor(n_tiles[:, :], base[:, :], key_start[:, :], ALU.subtract)
                drain()
                v.tensor_scalar(cnt_i[:, :], n_tiles[:, :], float(P - 1), None, ALU.add)
                drain()
                v.tensor_scalar(cnt_i[:, :], cnt_i[:, :], P.bit_length() - 1, None, ALU.arith_shift_right)
                v.tensor_copy(base[:, :], key_start[:, :])
                drain()
                v.tensor_copy(n_tiles[:, :], cnt_i[:, :])
                drain()
                v.tensor_tensor_scan(tiles_end[:, :], ones_e[:, :], n_tiles[:, :], 0.0, ALU.mult, ALU.add)
                drain()
                shape = [E, TC, E]
                v.tensor_tensor(cmp[:, :, :],
                                tiles_end[0:E, :].rearrange("p (a e) -> p a e", a=1).to_broadcast(shape),
                                tile_no[:, :].rearrange("p (c a) -> p c a", a=1).to_broadcast(shape), ALU.is_le)
                drain()
                v.tensor_reduce(t_exp[:, :], cmp[:, :, :], X, ALU.add)
                v.tensor_tensor(cmp2[:, :, :], cmp[:, :, :],
                                n_tiles[0:E, :].rearrange("p (a e) -> p a e", a=1).to_broadcast(shape), ALU.mult)
                drain()
                v.tensor_reduce(t_cst[:, :], cmp2[:, :, :], X, ALU.add)
                drain()
                v.tensor_tensor(t_cst[:, :], tile_no[:, :], t_cst[:, :], ALU.subtract)
                v.tensor_scalar(t_row[:, :], t_exp[:, :], float(CAP), None, ALU.mult)
                drain()
                v.scalar_tensor_tensor(out=t_row[:, :], in0=t_cst[:, :], scalar=float(P), in1=t_row[:, :],
                                       op0=ALU.mult, op1=ALU.add)
                v.tensor_scalar(t_exp[:, :], t_exp[:, :], float(E - 1), None, ALU.min)
                drain()
                for c in range(TC):
                    v.tensor_copy(cmp[:, c, :], t_row[:, c:c + 1].to_broadcast([E, E]))
                    last = v.tensor_copy(cmp2[:, c, :], t_exp[:, c:c + 1].to_broadcast([E, E]))
                last.then_inc(d_tab, 1)
                dve.wait_ge(p_tab, 2 * h + 1)
                span = slice(h * BT, (h + 1) * BT)
                v.tensor_scalar(own_key[0:E, span], M0[0:E, 0:BT], part1[0:E, 0:1], None, ALU.add)
                v.tensor_scalar(own_key[E:P, span], M0[0:E, 0:BT], part1[E:P, 0:1], None, ALU.add)
                v.tensor_copy(tile_row[0:1, span], M0[0:1, 0:BT]).then_inc(d_tabe, 1)
                dve.wait_ge(p_tab, 2 * h + 2)
                v.tensor_copy(tile_exp[0:1, span], M0[0:1, 0:BT]).then_inc(d_tabe, 1)

            def step(i2, p, first=False, last=False, half=False):
                g = 2 * i2 + p
                for u in range(G):
                    t = G * g + u
                    shift(t, 0)
                    shift(t, 1)
                    if not (first and u == 0):
                        attn_norm(t - 1)
                    if u == 0 and not last:
                        prep_norm(g + 1)
                    if u == 1:
                        if not last:
                            prep_keys(g + 1, 1 - p)
                        if not first:
                            route_norm(g - 1, i2 - 1 + p, 1 - p)
                    if u == 2 and not first:
                        route_groups(g - 1)
                    if u == 3 and not first:
                        route_top(g - 1)
                    if not (first and u == 0):
                        residual(t - 1)
                    if u == 3 and not first:
                        route_slots(g - 1, 1 - p)
                if half:
                    table(0)

            v.memset(ones_bf[:, :], 1.0)
            v.memset(ones_row[:, :], 1.0)
            v.memset(ones_e[:, :], 1.0)
            v.memset(pad_rows[:, 0:D + K], 0.0)
            v.memset(pad_rows[:, D + K:RW], FAR).then_inc(s_init, 1)
            for c in ctx_sb:
                v.memset(c[DC:DC + 1, :], 1.0)
            for c in v_aug:
                last = v.memset(c[:, :].rearrange("k (n c) -> k n c", c=DH + 1)[:, :, DH:DH + 1], 1.0)
            last.then_inc(s_vinit, 1)
            dve.wait_ge(s_const, 10)
            v.tensor_reduce(head_mask[:, :], head_bd[:, :].rearrange("p (i j) -> p j i", j=QH), X, ALU.add)
            v.tensor_copy(base[:, :], key_start[:, :])
            drain()
            dve.wait_ge(s_x, 16)
            prep_norm(0)
            prep_keys(0, 0)
            dve.wait_ge(s_xrest, 16)
            dve.wait_ge(s_w, 16 * 10)
            v.tensor_copy(wgu[:, :, I], gate_sb[:, :])
            step(0, 0, first=True)
            step(0, 1)
            with dve.Fori(1, HG // 2) as i2:
                step(i2, 0)
                step(i2, 1)
            step(HG // 2, 0, half=True)
            step(HG // 2, 1)
            with dve.Fori(HG // 2 + 1, NG // 2 - 1) as i2:
                step(i2, 0)
                step(i2, 1)
            step(NG // 2 - 1, 0)
            step(NG // 2 - 1, 1, last=True)
            attn_norm(NT - 1)
            residual(NT - 1)
            drain()
            route_norm(NG - 1, NG // 2 - 1, 1)
            route_groups(NG - 1)
            route_top(NG - 1)
            route_slots(NG - 1, 1)
            table(1)

            v.tensor_scalar(out_scale[:, :], score_sum[:, :], 1e-20, None, ALU.add)
            drain()
            v.reciprocal(out_scale[:, :], out_scale[:, :])
            drain()
            v.tensor_scalar(out_scale[:, :], out_scale[:, :], ROUTED_SCALE, None, ALU.mult)
            drain()

            h_v = b_h.rearrange("p (b u w) -> p b u w", b=2, u=2)

            def inner(j, p):
                dve.wait_ge(a_bsig, j + 1)
                v.tensor_tensor(h_v, b_sig[p][:, :, :, 0:I], PG[:, :, :, 0:I], ALU.mult)
                drain()
                v.tensor_tensor(h_v, h_v, PG[:, :, :, WG1:WGU], ALU.mult).then_inc(d_bh, 1)

            def places(i, q):
                j = STEPS * i + q
                r = q % RING
                dve.wait_ge(s_rin[r], 16 * G * (2 * i + (q // RING + 1)))
                if not (isinstance(i, int) and j < RING):
                    dve.wait_ge(s_ysc[r], 16 * G * (2 * i + q // RING))
                own = own_key[:, bass.ds(j * G, G)].rearrange("p (u a) -> p u a", a=1).to_broadcast([P, G, K])
                v.tensor_tensor(key_eq[:, :, :], rin[r][:, :, D:D + K], own, ALU.is_equal)
                drain()
                v.tensor_tensor(key_eq[:, :, :], key_eq[:, :, :],
                                rank8[:, :].rearrange("p (a k) -> p a k", a=1).to_broadcast([P, G, K]), ALU.mult)
                drain()
                v.tensor_reduce(key_rk[:, :], key_eq[:, :, :], X, ALU.add)
                drain()
                v.tensor_tensor(idx_ring[r][:, :], key_rk[:, :], rin[r][:, :, D + K], ALU.add)

            def scaled(i, q):
                j = STEPS * i + q
                dve.wait_ge(p_by, j + 1)
                sc = b_sig[q % 2].rearrange("p b u w -> p (b u) w")[:, :, I:WG1].to_broadcast([P, G, D])
                v.tensor_tensor(ring_y[q % RING], PY.rearrange("p (u d) -> p u d", d=D), sc,
                                ALU.mult).then_inc(d_by, 1)

            def expert_steps(i, last=False):
                for q in range(STEPS):
                    places(i, q)
                    scaled(i, q)
                    if not (last and q == STEPS - 1):
                        inner(STEPS * i + (q + 1), (q + 1) % 2)
                    if q in (3, 6):
                        a = (q - 3) // 3
                        dve.wait_ge(a_shsig, 2 * i + (a + 1))
                        v.tensor_tensor(sh_h[:, a, :], sh_sig[:, :], SHG[0:I, :], ALU.mult)
                        drain()
                        v.tensor_tensor(sh_h[:, a, :], sh_h[:, a, :], SHU[0:I, :], ALU.mult).then_inc(d_shh, 1)
                    if q == 8:
                        dve.wait_ge(p_sho, i + 1)
                        xt = xres[:, bass.ds(i * (G * D), G * D)]
                        v.tensor_tensor(xt, SHO, xt, ALU.add).then_inc(d_sho, 1)

            inner(0, 0)
            expert_steps(0)
            with dve.Fori(1, NG - 1) as i:
                expert_steps(i)
            expert_steps(NG - 1, last=True)
            drain()

            with dve.Fori(0, NG) as i:
                for r in range(G):
                    dve.wait_ge(s_cin[r], 16 * i + 16)
                    v.tensor_reduce(ao[:, :], c_ring[r].rearrange("p (k d) -> p d k", k=K), X, ALU.add)
                    drain()
                    xt = xres[:, bass.ds(i * (G * D) + r * D, D)]
                    v.scalar_tensor_tensor(out=xt, in0=ao[:, :], scalar=out_scale[:, bass.ds(i * G + r, 1)], in1=xt,
                                           op0=ALU.mult, op1=ALU.add).then_inc(d_fin, 1)
                    drain()

        @block.tensor
        def _(pe):
            mm = nc.tensor.matmul

            def prep_q(gp, p):
                pe.wait_ge(d_xn, gp + 1)
                for u in range(G):
                    last = nc.tensor.transpose(M0[:, u * P:(u + 1) * P], xn[:, u * D:(u + 1) * D], ident[:, :])
                last.then_inc(p_tr1, 1)
                pe.wait_ge(a_xnt, gp + 1)
                mm(M0, wq_sb[:, :], xn_t[:, :], start=True, stop=True).then_inc(p_q, 1)
                pe.wait_ge(a_q, gp + 1)

            def prep_k(gp, p, i2):
                pe.wait_ge(s_ctx[p], 16 * i2 + 16)
                mm(M0[:, 0:G * SK], wk_sb[:, :], ctx_sb[p][:, :], start=True, stop=True).then_inc(p_k, 1)

            def prep_v(gp, p):
                pe.wait_ge(d_bd, gp + 1)
                for u in range(G):
                    last = mm(M0[0:SK, u * D:(u + 1) * D], ctx_sb[p][:, u * SK:(u + 1) * SK], wv_sb[:, :],
                              start=True, stop=True)
                last.then_inc(p_v, 1)

            def scores(t, u, p):
                for h in range(2):
                    wait(pe, d_sub, 2 * t + (h - 1))
                    for b in range(2 * h, 2 * h + 2):
                        rws = slice(32 * b, 32 * b + 32)
                        last = mm(banks[:, b, 0:QH * SK], q_t[p][rws, u * P:(u + 1) * P],
                                  k_bd[p][rws, u * QH * SK:(u + 1) * QH * SK], start=True, stop=True)
                    last.then_inc(p_sc, 1)

            def rest(t, u, p, first):
                for i in range(4):
                    if i % 2 == 0:
                        pe.wait_ge(a_exp, 2 * t + (i // 2 + 1))
                    wait(pe, a_pt, 4 * t + (i - 1))
                    for j in range(4):
                        n = 4 * i + j
                        last = nc.tensor.transpose(T[i % 2][0:SK, j * P:(j + 1) * P],
                                                   probs[:, n * SK:(n + 1) * SK], ident[:, :])
                    last.then_inc(p_pt, 1)
                pe.wait_ge(a_pt, 4 * t + 4)
                wait(pe, d_res, t)
                w = DH + 1
                for n in range(NH):
                    last = mm(M1[:, n * w:(n + 1) * w], probs_t[0:SK, n * P:(n + 1) * P],
                              v_aug[p][:, (u * NH + n) * w:(u * NH + n + 1) * w], start=True, stop=True)
                last.then_inc(p_pv, 1)
                pe.wait_ge(d_ao, t + 1)
                nc.tensor.transpose(M1[:, 0:P], ao[:, :], ident[:, :]).then_inc(p_aot, 1)
                pe.wait_ge(a_aot, t + 1)
                mm(M1[:, P:2 * P], ao_t[:, :], wo_sb[:, :], start=True, stop=False)
                mm(M1[:, P:2 * P], ones_row[:, :], bo_sb[:, :], start=False, stop=True).then_inc(p_proj, 1)

            def logits(g, p, preps):
                pe.wait_ge(d_xn2, g + 1)
                pe.wait_ge(a_v, preps)
                for u in range(G):
                    last = nc.tensor.transpose(M0[:, u * P:(u + 1) * P], rows[p][:, u, 0:D], ident[:, :])
                last.then_inc(p_tr2, 1)
                pe.wait_ge(a_xn2t, g + 1)
                for u in range(G):
                    last = mm(M0[:, u * E:(u + 1) * E], xn2_t[p][:, u * P:(u + 1) * P], gate_sb[:, :],
                              start=True, stop=True)
                last.then_inc(p_logit, 1)

            def ranks(g):
                pe.wait_ge(a_es, g + 1)
                pe.wait_ge(d_chosen, g + 1)
                for u in range(G):
                    mm(M0[:, u * E:(u + 1) * E], upper[:, :], chosen[:, u, :], start=True, stop=(u == 0))
                    for b in range(u):
                        mm(M0[:, u * E:(u + 1) * E], ones_bf[:, :], chosen[:, b, :], start=False,
                           stop=(b == u - 1))
                for u in range(G):
                    last = mm(M0[:, G * E:(G + 1) * E], ones_bf[:, :], chosen[:, u, :], start=(u == 0),
                              stop=(u == G - 1))
                last.then_inc(p_rank, 1)

            def table(h):
                pe.wait_ge(d_tab, h + 1)
                for n, t in enumerate((cmp, cmp2)):
                    if n:
                        pe.wait_ge(d_tabe, 2 * h + 1)
                    for c in range(TC):
                        last = mm(M0[0:E, c * E:(c + 1) * E], t[:, c, :], ident[0:E, 0:E], start=True, stop=True)
                    last.then_inc(p_tab, 1)

            def step(i2, p, first=False, last=False, half=False):
                g = 2 * i2 + p
                for u in range(G):
                    t = G * g + u
                    if u == 0:
                        pe.wait_ge(a_q, g + 1)
                        pe.wait_ge(d_bd, g + 1)
                        pe.wait_ge(a_v, g + 1)
                    scores(t, u, p)
                    if not (first and u == 0):
                        rest(t - 1, (u - 1) % G, p if u else 1 - p, first)
                    if u == 0 and not last:
                        prep_q(g + 1, 1 - p)
                        prep_k(g + 1, 1 - p, i2 + p)
                    if u == 1:
                        if not last:
                            prep_v(g + 1, 1 - p)
                        if not first:
                            logits(g - 1, 1 - p, NG if last else g + 2)
                    if u == 3 and not first:
                        ranks(g - 1)
                if half:
                    table(0)

            pe.wait_ge(s_const, 10)
            pe.wait_ge(s_init, 1)
            pe.wait_ge(s_vinit, 1)
            pe.wait_ge(s_w, 16 * 10)
            prep_q(0, 0)
            prep_k(0, 0, 0)
            prep_v(0, 0)
            step(0, 0, first=True)
            step(0, 1)
            with pe.Fori(1, HG // 2) as i2:
                step(i2, 0)
                step(i2, 1)
            step(HG // 2, 0, half=True)
            step(HG // 2, 1)
            with pe.Fori(HG // 2 + 1, NG // 2 - 1) as i2:
                step(i2, 0)
                step(i2, 1)
            step(NG // 2 - 1, 0)
            step(NG // 2 - 1, 1, last=True)
            rest(NT - 1, G - 1, 1, False)
            logits(NG - 1, 1, NG)
            ranks(NG - 1)
            table(1)

            def turn(j, r, round_):
                pe.wait_ge(s_rin[r], 16 * G * round_)
                for u in range(G):
                    last = nc.tensor.transpose(PX[:, u * P:(u + 1) * P], rin[r][:, u, 0:D], ident[:, :])
                last.then_inc(p_bx, 1)

            def gate_up(j):
                ex = [pe.value_load(tile_exp[0:1, bass.ds(j * G + u, 1)], min_val=0, max_val=E - 1)
                      for u in range(G)]
                pe.wait_ge(a_bx, j + 1)
                wait(pe, d_bh, j)
                for u in range(G):
                    last = mm(banks[:, u // 2, (u % 2) * WGU:(u % 2 + 1) * WGU], b_xt[:, u * P:(u + 1) * P],
                              wgu[:, bass.ds(ex[u], 1), :], start=True, stop=True)
                last.then_inc(p_bgu, 1)
                return ex

            def down(j):
                ex = [pe.value_load(tile_exp[0:1, bass.ds(j * G + u, 1)], min_val=0, max_val=E - 1)
                      for u in range(G)]
                pe.wait_ge(a_bht, j + 1)
                for u in range(G):
                    last = mm(PY[:, u * D:(u + 1) * D], b_ht[0:I, u * P:(u + 1) * P],
                              wd[:, bass.ds(ex[u], 1), :], start=True, stop=True)
                last.then_inc(p_by, 1)

            def expert_steps(i, last_one=False):
                for q in range(STEPS):
                    j = STEPS * i + q
                    more = not (last_one and q == STEPS - 1)
                    if more:
                        turn(j + 1, (q + 1) % RING, 2 * i + ((q + 1) // RING + 1))
                    pe.wait_ge(d_bh, j + 1)
                    for u in range(G):
                        last = nc.tensor.transpose(PH[0:I, u * P:(u + 1) * P], b_h[:, u * I:(u + 1) * I],
                                                   ident[:, :])
                    last.then_inc(p_bht, 1)
                    if more:
                        gate_up(j + 1)
                    down(j)
                    if q in (2, 5):
                        a = (q - 2) // 3
                        if a == 0:
                            pe.wait_ge(s_shx, 16 * i + 16)
                        toks = sh_x[:, :]
                        mm(SHG[0:I, :], sg_w[:, a * I:(a + 1) * I], toks, start=True, stop=True)
                        mm(SHU[0:I, :], su_w[:, a * I:(a + 1) * I], toks, start=True, stop=True).then_inc(p_shgu, 1)
                    if q == 7:
                        pe.wait_ge(d_shh, 2 * i + 2)
                        for u in range(G):
                            for a in range(2):
                                last = mm(SHO[:, u * D:(u + 1) * D], sh_h[:, a, u * P:(u + 1) * P], sd_w[:, a, :],
                                          start=(a == 0), stop=(a == 1))
                        last.then_inc(p_sho, 1)

            pe.wait_ge(s_wexp, 16 * 6)
            pe.wait_ge(d_tabe, 4)
            turn(0, 0, 1)
            gate_up(0)
            with pe.Fori(0, NG - 1) as i:
                expert_steps(i)
            expert_steps(NG - 1, last_one=True)


_NAMES = ["x", "ctx_768", "wq", "bq", "wk", "bk", "wv", "bv", "wo", "bo", "gate_w", "gate_bias",
          "Wg", "Wu", "Wd", "Sg", "Su", "Sd"]


def kernel(**inputs):
    import numpy as _np
    import concourse.bacc as _bacc
    from concourse import mybir as _mybir
    from concourse.bass_utils import run_bass_kernel_spmd as _run

    a = {}
    for name in _NAMES:
        full = name if name in inputs else ("L0_xattn_" if "L0_xattn_" + name in inputs else "L0_ffn_") + name
        a[name] = _np.asarray(inputs[full])
    a["ctx_768"] = a["ctx_768"].transpose(2, 0, 1).reshape(DC, NT * SK)
    a["gate_w"] = a["gate_w"].T
    for name in ("Wg", "Wu"):
        a[name] = a[name].transpose(2, 0, 1)
    a["Wd"] = a["Wd"].transpose(2, 0, 1)
    for name in ("Sg", "Su", "Sd"):
        a[name] = a[name].T
    nc = _bacc.Bacc("TRN2", target_bir_lowering=False, num_devices=1)
    arrays, args = {}, []
    for name in _NAMES:
        arr = _np.ascontiguousarray(a[name])
        arrays[f"in_{name}"] = arr
        args.append(nc.dram_tensor(f"in_{name}", arr.shape, _mybir.dt.from_np(arr.dtype), kind="ExternalInput").ap())
    args.append(nc.dram_tensor("out_0", (NT, P, D), _mybir.dt.float32, kind="ExternalOutput").ap())
    moe_block(nc, *args)
    r = _run(nc, [arrays], core_ids=[0])
    return r.results[0]["out_0"]
```

```python
from contextlib import ExitStack

import concourse.bass as bass
from concourse import mybir

F32 = mybir.dt.float32
BF16 = mybir.dt.bfloat16
I32 = mybir.dt.int32
ALU = mybir.AluOpType
ACT = mybir.ActivationFunctionType
X = mybir.AxisListType.X

P = 128
NT = 64
D = 128
DC = 96
SK = 77
NH, DH = 16, 8
QH = 4
G = 4
NG = NT // G
E, I = 64, 88
EG = 8
TOPG = 4
K = 8
ROUTED_SCALE = 2.5
EPS = 1e-5
GUESS = float(0x5F3759DF)
HALVES = 2
HG = NG // HALVES
HT = NT * P // HALVES
CAP = HT + P
BT = HT * K // P + E
DUMMY = BT - HT * K // P
XROWS = E * CAP + DUMMY * P
RW = D + K + 1
TOKENS = NT * P
BG = BT // G
STEPS = HALVES * BG // NG
RING = 5
TC = BT // E
WG1 = I + 1
WGU = 2 * I + 1
FAR = 1.0e6
TAKEN = -3.0e38


def moe_block(nc, x, ctxt, wq, bq, wk, bk, wv, bv, wo, bo, gatet, gbias, wgt, wut, wdt, sgt, sut, sdt, out):
    ctx = ExitStack()
    with ctx:
        def sb(name, shape, dt=F32):
            return ctx.enter_context(nc.sbuf_tensor(name, shape, dt))

        def sem(name):
            return ctx.enter_context(nc.semaphore(name))

        routed_rows = [nc.dram_tensor(f"routed_rows{h}", [XROWS, RW], F32, kind="Internal").ap()
                       for h in range(HALVES)]
        normed_t = nc.dram_tensor("normed_t", [NG * P, G * P], F32, kind="Internal").ap()
        expert_out = nc.dram_tensor("expert_out", [TOKENS * K, D], F32, kind="Internal").ap()

        wq_sb = sb("wq_sb", [P, D])
        bq_sb = sb("bq_sb", [P, 1])
        wk_sb = sb("wk_sb", [DC + 1, D])
        wv_sb = sb("wv_sb", [DC + 1, D])
        wo_sb = sb("wo_sb", [P, D])
        bo_sb = sb("bo_sb", [1, D])
        gate_sb = sb("gate_sb", [P, E])
        gbias_sb = sb("gbias_sb", [P, E])
        wgu = sb("wgu", [P, E, WGU])
        wd = sb("wd", [I, E, D])
        sg_w = sb("sg_w", [P, 2 * I])
        su_w = sb("su_w", [P, 2 * I])
        sd_w = sb("sd_w", [I, 2, D])
        ident = sb("ident", [P, P])
        upper = sb("upper", [P, P], BF16)
        ones_bf = sb("ones_bf", [P, P], BF16)
        ones_row = sb("ones_row", [1, P])
        head_bd = sb("head_bd", [P, NH])
        head_mask = sb("head_mask", [P, QH])
        before = sb("before", [P, EG, EG])
        key_start = sb("key_start", [P, E])
        tok8 = sb("tok8", [P, NT])
        rank8 = sb("rank8", [P, K])
        part1 = sb("part1", [P, 1])
        tile_no = sb("tile_no", [E, TC])
        pad_rows = sb("pad_rows", [P, RW])
        ones_e = sb("ones_e", [P, E])

        xres = sb("xres", [P, NT * D])
        score_sum = sb("score_sum", [P, NT])
        out_scale = sb("out_scale", [P, NT])
        own_key = sb("own_key", [P, HALVES * BT])
        tile_row = sb("tile_row", [1, HALVES * BT], I32)
        tile_exp = sb("tile_exp", [1, HALVES * BT], I32)
        pad_row = sb("pad_row", [1, HALVES * E], I32)

        SCW = NH * SK
        arena = sb("arena", [P, 8200])
        at = [0]

        def carve(width):
            a = arena[:, at[0]:at[0] + width]
            at[0] += width
            assert at[0] <= 8200
            return a

        q_t = [carve(G * P) for _ in range(2)]
        k_bd = [carve(G * QH * SK) for _ in range(2)]
        shifted = carve(SCW)
        probs = carve(SCW)
        probs_t = carve(NH * P)
        at[0] = 0
        rin_f = [carve(G * RW) for _ in range(RING)]
        rin = [r.rearrange("p (u w) -> p u w", w=RW) for r in rin_f]
        ring_y = [carve(G * D).rearrange("p (u d) -> p u d", d=D) for _ in range(RING)]
        b_xt = carve(G * P)
        b_sig = [carve(G * WG1).rearrange("p (b u w) -> p b u w", b=2, u=2) for _ in range(2)]
        b_h = carve(G * I)
        b_ht = carve(G * P)

        ctx_sb = [sb(f"ctx_sb{i}", [DC + 1, G * SK]) for i in range(2)]
        v_aug = [sb(f"v_aug{i}", [SK, G * NH * (DH + 1)]) for i in range(2)]
        xn = sb("xn", [P, G * D])
        xn_t = sb("xn_t", [P, G * P])
        stats = sb("stats", [P, G, 6])
        mv = sb("mv", [P, G, 2])
        rstd = sb("rstd", [P, G])
        stats2 = sb("stats2", [P, G, 6])
        mv2 = sb("mv2", [P, G, 2])
        rstd2 = sb("rstd2", [P, G])
        var_eps = sb("var_eps", [P, G])
        var_half = sb("var_half", [P, G])
        guess = sb("guess", [P, G], I32)
        square = sb("square", [P, G])
        row_max = sb("row_max", [P, 2, 2, QH])
        rden = sb("rden", [P, NH])
        ao = sb("ao", [P, D])
        ao_t = sb("ao_t", [P, P])
        rows = [sb(f"rows{i}", [P, G, RW]) for i in range(2)]
        slots = [sb(f"slots{i}", [P, G, K], I32) for i in range(2)]
        xn2_t = [sb(f"xn2_t{i}", [P, G * P]) for i in range(2)]
        es = sb("es", [P, G, E])
        score = sb("score", [P, G, E])
        choice = sb("choice", [P, G, E])
        masked = sb("masked", [P, G, E])
        taken = sb("taken", [P, G, E])
        tmp = sb("tmp", [P, G, E])
        tmp2 = sb("tmp2", [P, G, E])
        hi4 = sb("hi4", [P, G * EG, 4])
        lo4 = sb("lo4", [P, G * EG, 4])
        hi2 = sb("hi2", [P, G * EG, 2])
        lo2 = sb("lo2", [P, G * EG, 2])
        mid2 = sb("mid2", [P, G * EG, 2])
        hi1 = sb("hi1", [P, G * EG])
        lo1 = sb("lo1", [P, G * EG])
        mid1 = sb("mid1", [P, G * EG])
        gscore = sb("gscore", [P, G, EG])
        gmask = sb("gmask", [P, G, EG])
        top8 = sb("top8", [P, G, K])
        chosen = sb("chosen", [P, G, E], BF16)
        base = sb("base", [P, E])
        cnt_i = sb("cnt_i", [P, E], I32)
        n_tiles = sb("n_tiles", [P, E])
        tiles_end = sb("tiles_end", [P, E])
        cmp = sb("cmp", [E, TC, E])
        cmp2 = sb("cmp2", [E, TC, E])
        t_exp = sb("t_exp", [E, TC])
        t_cst = sb("t_cst", [E, TC])
        t_row = sb("t_row", [E, TC])
        idx_ring = [sb(f"idx_ring{r}", [P, G], I32) for r in range(RING)]
        key_eq = sb("key_eq", [P, G, K])
        key_rk = sb("key_rk", [P, G])

        banks = ctx.enter_context(nc.psum_tensor("banks", [P, 8, 512], F32))
        T = [banks[:, 4, :], banks[:, 5, :]]
        M0 = banks[:, 6, :]
        M1 = banks[:, 7, :]
        PV = M1[:, 0:NH * (DH + 1)]
        AOT = M1[:, 0:P]
        PROJ = M1[:, P:2 * P]
        PX, PH, PY = banks[:, 4, :], banks[:, 5, :], banks[:, 2, :]
        PG = banks[:, 0:2, 0:2 * WGU].rearrange("p b (u w) -> p b u w", w=WGU)
        SHG, SHU, SHO = banks[:, 3, :], banks[:, 6, :], banks[:, 7, :]
        sh_x = sb("sh_x", [P, G * P])
        sh_sig = sb("sh_sig", [I, G * P])
        sh_h = sb("sh_h", [I, 2, G * P])

        c_ring = [wgu[:, :, :].rearrange("p e w -> p (e w)")[:, r * K * D:(r + 1) * K * D] for r in range(G)]

        s_x = sem("s_x")
        s_xrest = sem("s_xrest")
        s_w = sem("s_w")
        s_wexp = sem("s_wexp")
        s_ctx = [sem(f"s_ctx{i}") for i in range(2)]
        s_scat = [sem(f"s_scat{i}") for i in range(2)]
        s_pad = sem("s_pad")
        s_norm = [sem(f"s_norm{i}") for i in range(2)]
        s_shx = sem("s_shx")
        s_rin = [sem(f"s_rin{r}") for r in range(RING)]
        s_ysc = [sem(f"s_ysc{r}") for r in range(RING)]
        s_cin = [sem(f"s_cin{r}") for r in range(G)]
        s_out = sem("s_out")
        g_turn = sem("g_turn")
        s_const = sem("s_const")
        s_init = sem("s_init")
        s_vinit = sem("s_vinit")
        p_tr1 = sem("p_tr1")
        p_q = sem("p_q")
        p_k = sem("p_k")
        p_v = sem("p_v")
        p_sc = sem("p_sc")
        p_pt = sem("p_pt")
        p_pv = sem("p_pv")
        p_aot = sem("p_aot")
        p_proj = sem("p_proj")
        p_tr2 = sem("p_tr2")
        p_logit = sem("p_logit")
        p_rank = sem("p_rank")
        p_tab = sem("p_tab")
        p_bx = sem("p_bx")
        p_bgu = sem("p_bgu")
        p_bht = sem("p_bht")
        p_by = sem("p_by")
        p_shgu = sem("p_shgu")
        p_sho = sem("p_sho")
        a_xnt = sem("a_xnt")
        a_q = sem("a_q")
        a_v = sem("a_v")
        a_exp = sem("a_exp")
        a_pt = sem("a_pt")
        a_aot = sem("a_aot")
        a_xn2t = sem("a_xn2t")
        a_es = sem("a_es")
        a_bx = sem("a_bx")
        a_bht = sem("a_bht")
        a_bsig = sem("a_bsig")
        a_shsig = sem("a_shsig")
        d_xn = sem("d_xn")
        d_bd = sem("d_bd")
        d_sub = sem("d_sub")
        d_ao = sem("d_ao")
        d_res = sem("d_res")
        d_xn2 = sem("d_xn2")
        d_chosen = sem("d_chosen")
        d_slots = sem("d_slots")
        d_tab = sem("d_tab")
        d_tabe = sem("d_tabe")
        d_bh = sem("d_bh")
        d_by = sem("d_by")
        d_shh = sem("d_shh")
        d_sho = sem("d_sho")
        d_fin = sem("d_fin")

        def wait(eng, s, value):
            if not (isinstance(value, int) and value <= 0):
                eng.wait_ge(s, value)

        def read_four(eng, words, at, top):
            return nc.values_load_multi_w_load_instructions(
                words[0:1, bass.ds(at, G)], engines=[eng], min_val=0, max_val=top,
                skip_runtime_bounds_check_because="the table is worked out within these bounds")[1]

        def bank_scores(h):
            return banks[:, 2 * h:2 * h + 2, 0:QH * SK].rearrange("p b (j k) -> p b j k", k=SK)

        def half(t, h):
            return t[:, h * SCW // 2:(h + 1) * SCW // 2]

        block = ctx.enter_context(nc.Block())

        @block.sync
        def _(sp):
            x_v = x.rearrange("t p d -> p t d")
            xres_v = xres[:, :].rearrange("p (t d) -> p t d", d=D)
            sp.dma_start(xres_v[:, 0:G, :], x_v[:, 0:G, :]).then_inc(s_x, 16)
            sp.dma_start(wq_sb[:, :], wq).then_inc(s_w, 16)
            sp.dma_start(bq_sb[:, :], bq.rearrange("(p a) -> p a", a=1)).then_inc(s_w, 16)

            def load_ctx(i2, p):
                g = 2 * i2 + p
                wait(sp, p_v, g - 1)
                sp.dma_start(ctx_sb[p][0:DC, :], ctxt[:, bass.ds(g * (G * SK), G * SK)]).then_inc(s_ctx[p], 16)

            load_ctx(0, 0)
            load_ctx(0, 1)
            sp.dma_start(xres_v[:, G:NT, :], x_v[:, G:NT, :]).then_inc(s_xrest, 16)
            sp.dma_start(wgu[:, :, 0:I], wgt).then_inc(s_wexp, 16)
            sp.dma_start(wgu[:, :, WG1:WGU], wut).then_inc(s_wexp, 16)
            sp.dma_start(wd[:, :, :], wdt).then_inc(s_wexp, 16)
            sp.wait_ge(s_init, 1)
            for h in range(HALVES):
                sp.dma_start(routed_rows[h][E * CAP:XROWS, :].rearrange("(r p) w -> p r w", p=P),
                             pad_rows[:, :].rearrange("p (a w) -> p a w", a=1).to_broadcast([P, DUMMY, RW])
                             ).then_inc(s_pad, 16)

            def pads(h, i):
                ends = read_four(mybir.EngineType.SP, pad_row, i * G + h * E, E * CAP - P)
                for u in range(G):
                    sp.dma_start(routed_rows[h][bass.ds(ends[u], P), :], pad_rows[:, :]).then_inc(s_pad, 16)

            with sp.Fori(1, HG // 2 + 2) as i2:
                load_ctx(i2, 0)
                load_ctx(i2, 1)
            sp.wait_ge(d_tabe, 2)
            with sp.Fori(0, E // G) as i:
                pads(0, i)
            with sp.Fori(HG // 2 + 2, NG // 2) as i2:
                load_ctx(i2, 0)
                load_ctx(i2, 1)

            def load_shared(i):
                wait(sp, p_shgu, 2 * i)
                sp.dma_start(sh_x[:, :], normed_t[bass.ds(i * P, P), :]).then_inc(s_shx, 16)

            def load_rows(h, i, q):
                j = STEPS * i + q
                r = q % RING
                if not (isinstance(i, int) and j < RING):
                    sp.wait_ge(d_by, j - (RING - 1))
                    sp.wait_ge(p_bx, j - (RING - 1))
                first_rows = read_four(mybir.EngineType.SP, tile_row, j * G, XROWS - P)
                for u in range(G):
                    sp.dma_start(rin[r][:, u, :], routed_rows[h][bass.ds(first_rows[u], P), :]
                                 ).then_inc(s_rin[r], 16)

            sp.wait_ge(d_slots, HG + 2)
            sp.wait_ge(s_pad, 16 * (HALVES + E))
            sp.wait_ge(d_res, NT)
            for p in range(2):
                sp.wait_ge(s_norm[p], 16 * NG // 2)
            load_shared(0)
            for q in range(STEPS):
                load_rows(0, 0, q)
            sp.wait_ge(d_tabe, 4)
            pads(1, 0)
            pads(1, 1)
            with sp.Fori(1, NG // 2) as i:
                load_shared(i)
                for q in range(STEPS):
                    load_rows(0, i, q)
                    if q in (2, 7):
                        pads(1, 2 * i + q // 5)
            for p in range(2):
                sp.wait_ge(s_scat[p], 16 * G * K * NG // 2)
            sp.wait_ge(s_pad, 16 * (HALVES + 2 * E))
            with sp.Fori(NG // 2, NG) as i:
                load_shared(i)
                for q in range(STEPS):
                    load_rows(1, i, q)

            for r in range(RING):
                sp.wait_ge(s_ysc[r], 16 * G * HALVES * BG // RING)
            back = expert_out.rearrange("(n k) d -> n (k d)", k=K)

            def load_back(i, r):
                if not isinstance(i, int):
                    sp.wait_ge(d_fin, i * G + (r + 1 - G))
                sp.dma_start(c_ring[r], back[bass.ds((i * G + r) * P, P), :]).then_inc(s_cin[r], 16)

            for r in range(G):
                load_back(0, r)
            with sp.Fori(1, NG) as i:
                for r in range(G):
                    load_back(i, r)
            sp.wait_ge(s_out, 16 * NG)

        @block.gpsimd
        def _(pool):
            nc.gpsimd.memset(ident[:, :], 0.0).then_inc(s_const, 1)
            nc.gpsimd.memset(upper[:, :], 1.0).then_inc(s_const, 1)
            nc.gpsimd.memset(head_bd[:, :], 1.0).then_inc(s_const, 1)
            nc.gpsimd.memset(before[:, :, :], 1.0).then_inc(s_const, 1)
            pool.wait_ge(s_const, 4)
            nc.gpsimd.affine_select(out=ident[:, :], in_=ident[:, :], compare_op=ALU.not_equal, fill=1.0,
                                    base=0, pattern=[[-1, P]], channel_multiplier=1).then_inc(s_const, 1)
            nc.gpsimd.affine_select(out=upper[:, :], in_=upper[:, :], compare_op=ALU.is_gt, fill=0.0,
                                    base=0, pattern=[[1, P]], channel_multiplier=-1).then_inc(s_const, 1)
            nc.gpsimd.affine_select(out=head_bd[:, :], in_=head_bd[:, :], compare_op=ALU.is_ge, fill=0.0,
                                    base=0, pattern=[[-DH, NH]], channel_multiplier=1).then_inc(s_const, 1)
            nc.gpsimd.affine_select(out=before[:, :, :], in_=before[:, :, :], compare_op=ALU.is_gt, fill=0.0,
                                    base=0, pattern=[[1, EG], [-1, EG]], channel_multiplier=0).then_inc(s_const, 1)
            pool.wait_ge(s_const, 8)
            nc.gpsimd.affine_select(out=head_bd[:, :], in_=head_bd[:, :], compare_op=ALU.is_ge, fill=0.0,
                                    base=DH - 1, pattern=[[DH, NH]], channel_multiplier=-1).then_inc(s_const, 1)
            imprecise = dict(allow_small_or_imprecise_dtypes=True)
            nc.gpsimd.iota(key_start[:, :], [[CAP, E]], base=1, channel_multiplier=0, **imprecise)
            nc.gpsimd.iota(tok8[:, :], [[P * K, NT]], base=0, channel_multiplier=K, **imprecise)
            nc.gpsimd.iota(rank8[:, :], [[1, K]], base=0, channel_multiplier=0, **imprecise)
            nc.gpsimd.iota(part1[:, :], [[0, 1]], base=1, channel_multiplier=1, **imprecise)
            nc.gpsimd.iota(tile_no[:, :], [[E, TC]], base=0, channel_multiplier=1, **imprecise).then_inc(s_const, 1)

            def scatter(h, i2, p):
                pool.wait_ge(d_slots, 2 * i2 + (p + 1))
                pool.sem_inc(g_turn, 1)
                for u in range(G):
                    for k in range(K):
                        nc.gpsimd.indirect_dma_start(
                            out=routed_rows[h], out_offset=bass.IndirectOffsetOnAxis(ap=slots[p][:, u, k:k + 1], axis=0),
                            in_=rows[p][:, u, :], in_offset=None).then_inc(s_scat[p], 16)

            for h in range(HALVES):
                with pool.Fori(h * HG // 2, (h + 1) * HG // 2) as i2:
                    scatter(h, i2, 0)
                    scatter(h, i2, 1)
            with pool.Fori(0, NG) as i:
                for q in range(STEPS):
                    r = q % RING
                    pool.wait_ge(d_by, STEPS * i + (q + 1))
                    pool.sem_inc(g_turn, 1)
                    for u in range(G):
                        nc.gpsimd.indirect_dma_start(
                            out=expert_out, out_offset=bass.IndirectOffsetOnAxis(ap=idx_ring[r][:, u:u + 1], axis=0),
                            in_=ring_y[r][:, u, :], in_offset=None, bounds_check=TOKENS * K - 1,
                            oob_is_err=False).then_inc(s_ysc[r], 16)

        @block.scalar
        def _(act):
            act.dma_start(wk_sb[0:DC, :], wk).then_inc(s_w, 16)
            act.dma_start(wk_sb[DC:DC + 1, :], bk.rearrange("(a n) -> a n", a=1)).then_inc(s_w, 16)
            act.dma_start(wv_sb[0:DC, :], wv).then_inc(s_w, 16)
            act.dma_start(wv_sb[DC:DC + 1, :], bv.rearrange("(a n) -> a n", a=1)).then_inc(s_w, 16)
            act.dma_start(wo_sb[:, :], wo).then_inc(s_w, 16)
            act.dma_start(bo_sb[:, :], bo.rearrange("(a n) -> a n", a=1)).then_inc(s_w, 16)
            act.dma_start(gate_sb[:, :], gatet).then_inc(s_w, 16)
            act.dma_start(gbias_sb[:, :], gbias.rearrange("(a n) -> a n", a=1).to_broadcast([P, E])).then_inc(s_w, 16)
            act.dma_start(sg_w[:, :], sgt).then_inc(s_wexp, 16)
            act.dma_start(su_w[:, :], sut).then_inc(s_wexp, 16)
            act.dma_start(sd_w[:, :, :], sdt.rearrange("(a i) d -> i a d", i=I)).then_inc(s_wexp, 16)

            def normed_out(gp):
                act.wait_ge(p_tr1, gp + 1)
                nc.scalar.activation(xn_t[:, :], M0, ACT.Copy).then_inc(a_xnt, 1)

            def query_out(gp, p):
                act.wait_ge(p_q, gp + 1)
                nc.scalar.activation(q_t[p], M0, ACT.Identity, bias=bq_sb[:, 0:1]).then_inc(a_q, 1)

            def value_out(gp, p):
                act.wait_ge(p_v, gp + 1)
                if isinstance(gp, int) and gp < 2:
                    act.wait_ge(s_vinit, 1)
                dst = v_aug[p][:, :].rearrange("k (n c) -> k n c", c=DH + 1)[:, :, 0:DH]
                nc.scalar.activation(dst, M0[0:SK, :].rearrange("k (n c) -> k n c", c=DH), ACT.Copy).then_inc(a_v, 1)

            def probs_out(t, i):
                act.wait_ge(p_pt, 4 * t + (i + 1))
                nc.scalar.activation(probs_t[0:SK, i * 512:(i + 1) * 512], T[i % 2][0:SK, :],
                                     ACT.Copy).then_inc(a_pt, 1)

            def exp(t, h):
                act.wait_ge(d_sub, 2 * t + (h + 1))
                nc.scalar.activation(half(probs, h), half(shifted, h), ACT.Exp,
                                     scale=float(DH) ** -0.5).then_inc(a_exp, 1)

            def attn_t(t):
                act.wait_ge(p_aot, t + 1)
                nc.scalar.activation(ao_t[:, :], AOT, ACT.Copy).then_inc(a_aot, 1)

            def normed2_out(g, i2, p):
                act.wait_ge(p_tr2, g + 1)
                wait(act, s_norm[p], 16 * i2)
                nc.scalar.activation(xn2_t[p][:, :], M0, ACT.Copy).then_inc(a_xn2t, 1)

            def logits_out(g, p):
                act.wait_ge(p_logit, g + 1)
                nc.scalar.activation(es[:, :, :], M0[:, 0:G * E].rearrange("p (u e) -> p u e", e=E), ACT.Exp,
                                     scale=-1.0).then_inc(a_es, 1)
                act.wait_ge(a_xn2t, g + 1)
                act.dma_start(normed_t[bass.ds(g * P, P), :], xn2_t[p][:, :]).then_inc(s_norm[p], 16)

            def slot(t, u, g, i2, p, one_back=True, two_back=True, scores=True, nextp=True, route=True):
                if u == 2 and nextp:
                    value_out(g + 1, 1 - p)
                if two_back:
                    attn_t(t - 2)
                if one_back:
                    probs_out(t - 1, 0)
                    probs_out(t - 1, 1)
                if scores:
                    exp(t, 0)
                if one_back:
                    probs_out(t - 1, 2)
                if u == 1 and nextp:
                    query_out(g + 1, 1 - p)
                if one_back:
                    probs_out(t - 1, 3)
                if u == 2 and route:
                    normed2_out(g - 1, i2 - 1 + p, 1 - p)
                if scores:
                    exp(t, 1)
                if u == 0 and nextp:
                    normed_out(g + 1)
                if u == 2 and route:
                    logits_out(g - 1, 1 - p)

            def step(i2, p, first=False, last=False):
                g = 2 * i2 + p
                for u in range(G):
                    slot(G * g + u, u, g, i2, p, one_back=not first or u > 0, two_back=not first or u > 1,
                         nextp=not last, route=not first)

            normed_out(0)
            query_out(0, 0)
            value_out(0, 0)
            step(0, 0, first=True)
            step(0, 1)
            step(1, 0)
            step(1, 1)
            with act.Fori(2, NG // 2 - 1) as i2:
                step(i2, 0)
                step(i2, 1)
            step(NG // 2 - 1, 0)
            step(NG // 2 - 1, 1, last=True)
            slot(NT, 0, NG, NG // 2, 0, scores=False, nextp=False)
            slot(NT + 1, 1, NG, NG // 2, 0, one_back=False, scores=False, nextp=False)
            normed2_out(NG - 1, NG // 2 - 1, 1)
            logits_out(NG - 1, 1)

            def front(j, p):
                act.wait_ge(p_bx, j + 1)
                nc.scalar.activation(b_xt, PX, ACT.Copy).then_inc(a_bx, 1)
                act.wait_ge(p_bgu, j + 1)
                nc.scalar.activation(b_sig[p], PG[:, :, :, 0:WG1], ACT.Sigmoid).then_inc(a_bsig, 1)

            def expert_steps(i, last=False):
                for q in range(STEPS):
                    j = STEPS * i + q
                    more = not (last and q == STEPS - 1)
                    if more:
                        act.wait_ge(p_bx, j + 2)
                        nc.scalar.activation(b_xt, PX, ACT.Copy).then_inc(a_bx, 1)
                    act.wait_ge(p_bht, j + 1)
                    nc.scalar.activation(b_ht[0:I, :], PH[0:I, :], ACT.Copy).then_inc(a_bht, 1)
                    if more:
                        act.wait_ge(p_bgu, j + 2)
                        wait(act, d_by, j)
                        nc.scalar.activation(b_sig[(q + 1) % 2], PG[:, :, :, 0:WG1], ACT.Sigmoid).then_inc(a_bsig, 1)
                    if q in (3, 6):
                        a = (q - 3) // 3
                        act.wait_ge(p_shgu, 2 * i + (a + 1))
                        nc.scalar.activation(sh_sig[:, :], SHG[0:I, :], ACT.Sigmoid).then_inc(a_shsig, 1)

            front(0, 0)
            expert_steps(0)
            with act.Fori(1, NG - 1) as i:
                expert_steps(i)
            expert_steps(NG - 1, last=True)

            def store(i):
                act.wait_ge(d_fin, G * i + G)
                act.dma_start(out[bass.ds(i * G, G), :, :].rearrange("t p d -> p t d"),
                              xres[:, bass.ds(i * (G * D), G * D)].rearrange("p (t d) -> p t d", d=D)
                              ).then_inc(s_out, 16)

            with act.Fori(0, NG) as i:
                store(i)
            act.wait_ge(s_out, 16 * NG)

        @block.vector
        def _(dve):
            v = nc.vector

            def drain():
                dve.drain()

            def norm(src_group, dst, st, m, r, ready):
                for u in range(G):
                    v.bn_stats(st[:, u, :], xres[:, bass.ds(src_group * (G * D) + u * D, D)])
                drain()
                for u in range(G):
                    v.bn_aggr(m[:, u, :], st[:, u, :])
                drain()
                v.tensor_scalar(var_eps[:, :], m[:, :, 1], EPS, None, ALU.add)
                v.tensor_scalar(var_half[:, :], m[:, :, 1], -0.5, -0.5 * EPS, ALU.mult, ALU.add)
                drain()
                v.tensor_scalar(guess[:, :], var_eps[:, :].bitcast(I32), 1, None, ALU.arith_shift_right)
                drain()
                v.tensor_scalar(r[:, :].bitcast(I32), guess[:, :], -1.0, GUESS, ALU.mult, ALU.add)
                drain()
                for _ in range(3):
                    v.tensor_tensor(square[:, :], r[:, :], r[:, :], ALU.mult)
                    drain()
                    v.tensor_tensor(square[:, :], square[:, :], var_half[:, :], ALU.mult)
                    drain()
                    v.scalar_tensor_tensor(out=r[:, :], in0=square[:, :], scalar=1.5, in1=r[:, :],
                                           op0=ALU.add, op1=ALU.mult)
                    drain()
                for u in range(G):
                    last = v.tensor_scalar(dst(u), xres[:, bass.ds(src_group * (G * D) + u * D, D)],
                                           m[:, u, 0:1], r[:, u:u + 1], ALU.subtract, ALU.mult)
                last.then_inc(ready, 1)

            def prep_norm(gp):
                wait(dve, p_tr1, gp)
                norm(gp, lambda u: xn[:, u * D:(u + 1) * D], stats, mv, rstd, d_xn)

            def prep_keys(gp, p):
                dve.wait_ge(p_k, gp + 1)
                v.tensor_tensor(
                    k_bd[p].rearrange("p (u j k) -> p u j k", u=G, j=QH),
                    M0[:, 0:G * SK].rearrange("p (u a k) -> p u a k", u=G, a=1).to_broadcast([P, G, QH, SK]),
                    head_mask[:, :].rearrange("p (a j b) -> p a j b", a=1, b=1).to_broadcast([P, G, QH, SK]),
                    ALU.mult).then_inc(d_bd, 1)

            def shift(t, h):
                dve.wait_ge(p_sc, 2 * t + (h + 1))
                v.tensor_reduce(row_max[:, h, :, :], bank_scores(h), X, ALU.max)
                drain()
                wait(dve, a_exp, 2 * t + (h - 1))
                v.tensor_tensor(half(shifted, h).rearrange("p (b j k) -> p b j k", b=2, k=SK), bank_scores(h),
                                row_max[:, h, :, :].rearrange("p b (j a) -> p b j a", a=1).to_broadcast([P, 2, QH, SK]),
                                ALU.subtract).then_inc(d_sub, 1)

            def attn_norm(t):
                dve.wait_ge(p_pv, t + 1)
                pv = PV.rearrange("p (n c) -> p n c", c=DH + 1)
                v.reciprocal(rden[:, :], pv[:, :, DH])
                drain()
                v.tensor_tensor(ao[:, :].rearrange("p (n c) -> p n c", c=DH), pv[:, :, 0:DH],
                                rden[:, :].rearrange("p (n a) -> p n a", a=1).to_broadcast([P, NH, DH]),
                                ALU.mult).then_inc(d_ao, 1)

            def residual(t):
                dve.wait_ge(p_proj, t + 1)
                xt = xres[:, bass.ds(t * D, D)]
                v.tensor_tensor(xt, PROJ, xt, ALU.add).then_inc(d_res, 1)

            def route_norm(g, i2, p):
                wait(dve, s_scat[p], 16 * G * K * i2)
                norm(g, lambda u: rows[p][:, u, 0:D], stats2, mv2, rstd2, d_xn2)
                v.tensor_copy(rows[p][:, :, D + K], tok8[:, bass.ds(g * G, G)])

            def route_groups(g):
                dve.wait_ge(a_es, g + 1)
                v.tensor_scalar(tmp[:, :, :], es[:, :, :], 1.0, None, ALU.add)
                drain()
                v.reciprocal(score[:, :, :], tmp[:, :, :])
                drain()
                v.tensor_tensor(choice[:, :, :], score[:, :, :],
                                gbias_sb[:, :].rearrange("p (a e) -> p a e", a=1).to_broadcast([P, G, E]), ALU.add)
                drain()
                cg = choice[:, :, :].rearrange("p u (g k) -> p (u g) k", k=EG)
                v.tensor_tensor(hi4[:, :, :], cg[:, :, 0:4], cg[:, :, 4:8], ALU.max)
                v.tensor_tensor(lo4[:, :, :], cg[:, :, 0:4], cg[:, :, 4:8], ALU.min)
                drain()
                v.tensor_tensor(hi2[:, :, :], hi4[:, :, 0:2], hi4[:, :, 2:4], ALU.max)
                v.tensor_tensor(mid2[:, :, :], hi4[:, :, 0:2], hi4[:, :, 2:4], ALU.min)
                v.tensor_tensor(lo2[:, :, :], lo4[:, :, 0:2], lo4[:, :, 2:4], ALU.max)
                drain()
                v.tensor_tensor(lo2[:, :, :], lo2[:, :, :], mid2[:, :, :], ALU.max)
                v.tensor_tensor(hi1[:, :], hi2[:, :, 0], hi2[:, :, 1], ALU.max)
                v.tensor_tensor(mid1[:, :], hi2[:, :, 0], hi2[:, :, 1], ALU.min)
                drain()
                v.tensor_tensor(lo1[:, :], lo2[:, :, 0], lo2[:, :, 1], ALU.max)
                drain()
                v.tensor_tensor(lo1[:, :], lo1[:, :], mid1[:, :], ALU.max)
                drain()
                v.tensor_tensor(gscore[:, :, :].rearrange("p u g -> p (u g)"), hi1[:, :], lo1[:, :], ALU.add)
                drain()
                gi = gscore[:, :, :].rearrange("p u (i a) -> p u i a", a=1).to_broadcast([P, G, EG, EG])
                gj = gscore[:, :, :].rearrange("p u (a j) -> p u a j", a=1).to_broadcast([P, G, EG, EG])
                t4 = tmp[:, :, :].rearrange("p u (i j) -> p u i j", j=EG)
                u4 = tmp2[:, :, :].rearrange("p u (i j) -> p u i j", j=EG)
                v.tensor_tensor(t4, gj, gi, ALU.is_gt)
                v.tensor_tensor(u4, gj, gi, ALU.is_equal)
                drain()
                bef = before[:, :, :].rearrange("p i (a j) -> p a i j", a=1).to_broadcast([P, G, EG, EG])
                v.tensor_tensor(u4, u4, bef, ALU.mult)
                drain()
                v.tensor_tensor(t4, t4, u4, ALU.add)
                drain()
                v.tensor_reduce(gmask[:, :, :], t4, X, ALU.add)
                drain()
                v.tensor_scalar(gmask[:, :, :], gmask[:, :, :], float(TOPG), None, ALU.is_lt)
                drain()
                v.tensor_tensor(masked[:, :, :].rearrange("p u (g k) -> p (u g) k", k=EG), cg,
                                gmask[:, :, :].rearrange("p u (g a) -> p (u g) a", a=1).to_broadcast([P, G * EG, EG]),
                                ALU.mult)
                drain()

            def route_top(g):
                for u in range(G):
                    v.max(top8[:, u, :], masked[:, u, :])
                drain()
                for u in range(G):
                    v.match_replace(out=taken[:, u, :], in_to_replace=top8[:, u, :], in_values=masked[:, u, :],
                                    imm_value=TAKEN)
                drain()
                v.tensor_scalar(chosen[:, :, :], taken[:, :, :], TAKEN / 2, None, ALU.is_lt).then_inc(d_chosen, 1)
                drain()

            def route_sum(g):
                v.tensor_tensor(tmp[:, :, :], score[:, :, :], chosen[:, :, :], ALU.mult)
                drain()
                v.tensor_reduce(score_sum[:, bass.ds(g * G, G)], tmp[:, :, :], X, ALU.add)

            def route_slots(g, p):
                dve.wait_ge(p_rank, g + 1)
                rk = M0[:, 0:G * E].rearrange("p (u e) -> p u e", e=E)
                v.tensor_tensor(tmp2[:, :, :], rk,
                                base[:, :].rearrange("p (a e) -> p a e", a=1).to_broadcast([P, G, E]), ALU.add)
                drain()
                v.tensor_tensor(base[:, :], M0[:, G * E:G * E + E], base[:, :], ALU.add)
                v.tensor_tensor(tmp2[:, :, :], tmp2[:, :, :], chosen[:, :, :], ALU.mult)
                drain()
                for u in range(G):
                    v.max(rows[p][:, u, D:D + K], tmp2[:, u, :])
                drain()
                v.tensor_scalar(slots[p][:, :, :], rows[p][:, :, D:D + K], -1.0, None,
                                ALU.add).then_inc(d_slots, 1)

            def table(h):
                v.tensor_scalar(pad_row[0:1, h * E:(h + 1) * E], base[0:1, :], -1.0, None, ALU.add)
                v.tensor_tensor(n_tiles[:, :], base[:, :], key_start[:, :], ALU.subtract)
                drain()
                v.tensor_scalar(cnt_i[:, :], n_tiles[:, :], float(P - 1), None, ALU.add)
                drain()
                v.tensor_scalar(cnt_i[:, :], cnt_i[:, :], P.bit_length() - 1, None, ALU.arith_shift_right)
                v.tensor_copy(base[:, :], key_start[:, :])
                drain()
                v.tensor_copy(n_tiles[:, :], cnt_i[:, :])
                drain()
                v.tensor_tensor_scan(tiles_end[:, :], ones_e[:, :], n_tiles[:, :], 0.0, ALU.mult, ALU.add)
                drain()
                shape = [E, TC, E]
                v.tensor_tensor(cmp[:, :, :],
                                tiles_end[0:E, :].rearrange("p (a e) -> p a e", a=1).to_broadcast(shape),
                                tile_no[:, :].rearrange("p (c a) -> p c a", a=1).to_broadcast(shape), ALU.is_le)
                drain()
                v.tensor_reduce(t_exp[:, :], cmp[:, :, :], X, ALU.add)
                v.tensor_tensor(cmp2[:, :, :], cmp[:, :, :],
                                n_tiles[0:E, :].rearrange("p (a e) -> p a e", a=1).to_broadcast(shape), ALU.mult)
                drain()
                v.tensor_reduce(t_cst[:, :], cmp2[:, :, :], X, ALU.add)
                drain()
                v.tensor_tensor(t_cst[:, :], tile_no[:, :], t_cst[:, :], ALU.subtract)
                v.tensor_scalar(t_row[:, :], t_exp[:, :], float(CAP), None, ALU.mult)
                drain()
                v.scalar_tensor_tensor(out=t_row[:, :], in0=t_cst[:, :], scalar=float(P), in1=t_row[:, :],
                                       op0=ALU.mult, op1=ALU.add)
                v.tensor_scalar(t_exp[:, :], t_exp[:, :], float(E - 1), None, ALU.min)
                drain()
                for c in range(TC):
                    v.tensor_copy(cmp[:, c, :], t_row[:, c:c + 1].to_broadcast([E, E]))
                    last = v.tensor_copy(cmp2[:, c, :], t_exp[:, c:c + 1].to_broadcast([E, E]))
                last.then_inc(d_tab, 1)
                dve.wait_ge(p_tab, 2 * h + 1)
                span = slice(h * BT, (h + 1) * BT)
                v.tensor_scalar(own_key[0:E, span], M0[0:E, 0:BT], part1[0:E, 0:1], None, ALU.add)
                v.tensor_scalar(own_key[E:P, span], M0[0:E, 0:BT], part1[E:P, 0:1], None, ALU.add)
                v.tensor_copy(tile_row[0:1, span], M0[0:1, 0:BT]).then_inc(d_tabe, 1)
                dve.wait_ge(p_tab, 2 * h + 2)
                v.tensor_copy(tile_exp[0:1, span], M0[0:1, 0:BT]).then_inc(d_tabe, 1)

            def step(i2, p, groups_behind=2, last=False, half=False, more_norm=True):
                g = 2 * i2 + p
                for u in range(G):
                    t = G * g + u
                    two_back = groups_behind > 0 or u > 1
                    if two_back:
                        attn_norm(t - 2)
                    shift(t, 0)
                    shift(t, 1)
                    if two_back:
                        residual(t - 2)
                    if u == 1 and not last:
                        prep_keys(g + 1, 1 - p)
                    if u == 0 and groups_behind > 1:
                        route_slots(g - 2, p)
                        route_sum(g - 2)
                    if u == 1 and groups_behind > 0:
                        drain()
                        route_norm(g - 1, i2 - 1 + p, 1 - p)
                    if u == 2 and more_norm:
                        prep_norm(g + 2)
                    if u == 3 and groups_behind > 0:
                        route_groups(g - 1)
                        route_top(g - 1)
                if half:
                    table(0)

            v.memset(ones_bf[:, :], 1.0)
            v.memset(ones_row[:, :], 1.0)
            v.memset(ones_e[:, :], 1.0)
            v.memset(pad_rows[:, 0:D + K], 0.0)
            v.memset(pad_rows[:, D + K:RW], FAR).then_inc(s_init, 1)
            for c in ctx_sb:
                v.memset(c[DC:DC + 1, :], 1.0)
            for c in v_aug:
                last = v.memset(c[:, :].rearrange("k (n c) -> k n c", c=DH + 1)[:, :, DH:DH + 1], 1.0)
            last.then_inc(s_vinit, 1)
            dve.wait_ge(s_const, 10)
            v.tensor_reduce(head_mask[:, :], head_bd[:, :].rearrange("p (i j) -> p j i", j=QH), X, ALU.add)
            v.tensor_copy(base[:, :], key_start[:, :])
            drain()
            dve.wait_ge(s_x, 16)
            prep_norm(0)
            prep_keys(0, 0)
            dve.wait_ge(s_xrest, 16)
            prep_norm(1)
            dve.wait_ge(s_w, 16 * 10)
            v.tensor_copy(wgu[:, :, I], gate_sb[:, :])
            step(0, 0, groups_behind=0)
            step(0, 1, groups_behind=1)
            step(1, 0)
            step(1, 1)
            with dve.Fori(2, HG // 2) as i2:
                step(i2, 0)
                step(i2, 1)
            step(HG // 2, 0)
            step(HG // 2, 1, half=True)
            with dve.Fori(HG // 2 + 1, NG // 2 - 1) as i2:
                step(i2, 0)
                step(i2, 1)
            step(NG // 2 - 1, 0, more_norm=False)
            step(NG // 2 - 1, 1, last=True, more_norm=False)
            attn_norm(NT - 2)
            residual(NT - 2)
            route_slots(NG - 2, 0)
            route_sum(NG - 2)
            attn_norm(NT - 1)
            residual(NT - 1)
            drain()
            route_norm(NG - 1, NG // 2 - 1, 1)
            route_groups(NG - 1)
            route_top(NG - 1)
            route_slots(NG - 1, 1)
            route_sum(NG - 1)
            table(1)

            v.tensor_scalar(out_scale[:, :], score_sum[:, :], 1e-20, None, ALU.add)
            drain()
            v.reciprocal(out_scale[:, :], out_scale[:, :])
            drain()
            v.tensor_scalar(out_scale[:, :], out_scale[:, :], ROUTED_SCALE, None, ALU.mult)
            drain()

            h_v = b_h.rearrange("p (b u w) -> p b u w", b=2, u=2)

            def inner(j, p):
                dve.wait_ge(a_bsig, j + 1)
                v.tensor_tensor(h_v, b_sig[p][:, :, :, 0:I], PG[:, :, :, 0:I], ALU.mult)
                drain()
                v.tensor_tensor(h_v, h_v, PG[:, :, :, WG1:WGU], ALU.mult).then_inc(d_bh, 1)

            def places(i, q):
                j = STEPS * i + q
                r = q % RING
                dve.wait_ge(s_rin[r], 16 * G * (2 * i + (q // RING + 1)))
                if not (isinstance(i, int) and j < RING):
                    dve.wait_ge(s_ysc[r], 16 * G * (2 * i + q // RING))
                own = own_key[:, bass.ds(j * G, G)].rearrange("p (u a) -> p u a", a=1).to_broadcast([P, G, K])
                v.tensor_tensor(key_eq[:, :, :], rin[r][:, :, D:D + K], own, ALU.is_equal)
                drain()
                v.tensor_tensor(key_eq[:, :, :], key_eq[:, :, :],
                                rank8[:, :].rearrange("p (a k) -> p a k", a=1).to_broadcast([P, G, K]), ALU.mult)
                drain()
                v.tensor_reduce(key_rk[:, :], key_eq[:, :, :], X, ALU.add)
                drain()
                v.tensor_tensor(idx_ring[r][:, :], key_rk[:, :], rin[r][:, :, D + K], ALU.add)

            def scaled(i, q):
                j = STEPS * i + q
                dve.wait_ge(p_by, j + 1)
                sc = b_sig[q % 2].rearrange("p b u w -> p (b u) w")[:, :, I:WG1].to_broadcast([P, G, D])
                v.tensor_tensor(ring_y[q % RING], PY.rearrange("p (u d) -> p u d", d=D), sc,
                                ALU.mult).then_inc(d_by, 1)

            def expert_steps(i, last=False):
                for q in range(STEPS):
                    places(i, q)
                    if not (last and q == STEPS - 1):
                        inner(STEPS * i + (q + 1), (q + 1) % 2)
                    scaled(i, q)
                    if q in (3, 6):
                        a = (q - 3) // 3
                        dve.wait_ge(a_shsig, 2 * i + (a + 1))
                        v.tensor_tensor(sh_h[:, a, :], sh_sig[:, :], SHG[0:I, :], ALU.mult)
                        drain()
                        v.tensor_tensor(sh_h[:, a, :], sh_h[:, a, :], SHU[0:I, :], ALU.mult).then_inc(d_shh, 1)
                    if q == 8:
                        dve.wait_ge(p_sho, i + 1)
                        xt = xres[:, bass.ds(i * (G * D), G * D)]
                        v.tensor_tensor(xt, SHO, xt, ALU.add).then_inc(d_sho, 1)

            inner(0, 0)
            expert_steps(0)
            with dve.Fori(1, NG - 1) as i:
                expert_steps(i)
            expert_steps(NG - 1, last=True)
            drain()

            with dve.Fori(0, NG) as i:
                for r in range(G):
                    dve.wait_ge(s_cin[r], 16 * i + 16)
                    v.tensor_reduce(ao[:, :], c_ring[r].rearrange("p (k d) -> p d k", k=K), X, ALU.add)
                    drain()
                    xt = xres[:, bass.ds(i * (G * D) + r * D, D)]
                    v.scalar_tensor_tensor(out=xt, in0=ao[:, :], scalar=out_scale[:, bass.ds(i * G + r, 1)], in1=xt,
                                           op0=ALU.mult, op1=ALU.add).then_inc(d_fin, 1)
                    drain()

        @block.tensor
        def _(pe):
            mm = nc.tensor.matmul

            def prep_tokens(gp):
                pe.wait_ge(d_xn, gp + 1)
                if not isinstance(gp, int) or gp > 2:
                    pe.wait_ge(d_slots, gp - 2)
                elif gp:
                    pe.wait_ge(a_v, gp)
                for u in range(G):
                    last = nc.tensor.transpose(M0[:, u * P:(u + 1) * P], xn[:, u * D:(u + 1) * D], ident[:, :])
                last.then_inc(p_tr1, 1)

            def prep_q(gp):
                pe.wait_ge(a_xnt, gp + 1)
                mm(M0, wq_sb[:, :], xn_t[:, :], start=True, stop=True).then_inc(p_q, 1)

            def prep_k(gp, p, i2):
                pe.wait_ge(a_q, gp + 1)
                pe.wait_ge(s_ctx[p], 16 * i2 + 16)
                mm(M0[:, 0:G * SK], wk_sb[:, :], ctx_sb[p][:, :], start=True, stop=True).then_inc(p_k, 1)

            def prep_v(gp, p):
                pe.wait_ge(d_bd, gp + 1)
                for u in range(G):
                    last = mm(M0[0:SK, u * D:(u + 1) * D], ctx_sb[p][:, u * SK:(u + 1) * SK], wv_sb[:, :],
                              start=True, stop=True)
                last.then_inc(p_v, 1)

            def scores(t, u, p):
                for h in range(2):
                    wait(pe, d_sub, 2 * t + (h - 1))
                    for b in range(2 * h, 2 * h + 2):
                        rws = slice(32 * b, 32 * b + 32)
                        last = mm(banks[:, b, 0:QH * SK], q_t[p][rws, u * P:(u + 1) * P],
                                  k_bd[p][rws, u * QH * SK:(u + 1) * QH * SK], start=True, stop=True)
                    last.then_inc(p_sc, 1)

            def probs_across(t, i):
                if i % 2 == 0:
                    pe.wait_ge(a_exp, 2 * t + (i // 2 + 1))
                wait(pe, a_pt, 4 * t + (i - 1))
                for j in range(4):
                    n = 4 * i + j
                    last = nc.tensor.transpose(T[i % 2][0:SK, j * P:(j + 1) * P],
                                               probs[:, n * SK:(n + 1) * SK], ident[:, :])
                last.then_inc(p_pt, 1)

            def weighted_values(t, u, p, i):
                if i == 0:
                    wait(pe, d_res, t)
                pe.wait_ge(a_pt, 4 * t + (i + 1))
                w = DH + 1
                for n in range(4 * i, 4 * i + 4):
                    last = mm(PV[:, n * w:(n + 1) * w], probs_t[0:SK, n * P:(n + 1) * P],
                              v_aug[p][:, (u * NH + n) * w:(u * NH + n + 1) * w], start=True, stop=True)
                if i == 3:
                    last.then_inc(p_pv, 1)

            def attn_across(t):
                pe.wait_ge(d_ao, t + 1)
                nc.tensor.transpose(AOT, ao[:, :], ident[:, :]).then_inc(p_aot, 1)

            def project(t):
                pe.wait_ge(a_aot, t + 1)
                mm(PROJ, ao_t[:, :], wo_sb[:, :], start=True, stop=False)
                mm(PROJ, ones_row[:, :], bo_sb[:, :], start=False, stop=True).then_inc(p_proj, 1)

            def normed2_across(g, p, preps):
                pe.wait_ge(d_xn2, g + 1)
                pe.wait_ge(a_v, preps)
                for u in range(G):
                    last = nc.tensor.transpose(M0[:, u * P:(u + 1) * P], rows[p][:, u, 0:D], ident[:, :])
                last.then_inc(p_tr2, 1)

            def logits(g, p):
                pe.wait_ge(a_xn2t, g + 1)
                for u in range(G):
                    last = mm(M0[:, u * E:(u + 1) * E], xn2_t[p][:, u * P:(u + 1) * P], gate_sb[:, :],
                              start=True, stop=True)
                last.then_inc(p_logit, 1)

            def ranks(g):
                pe.wait_ge(a_es, g + 1)
                pe.wait_ge(d_chosen, g + 1)
                for u in range(G):
                    mm(M0[:, u * E:(u + 1) * E], upper[:, :], chosen[:, u, :], start=True, stop=(u == 0))
                    for b in range(u):
                        mm(M0[:, u * E:(u + 1) * E], ones_bf[:, :], chosen[:, b, :], start=False,
                           stop=(b == u - 1))
                for u in range(G):
                    last = mm(M0[:, G * E:(G + 1) * E], ones_bf[:, :], chosen[:, u, :], start=(u == 0),
                              stop=(u == G - 1))
                last.then_inc(p_rank, 1)

            def table(h):
                pe.wait_ge(d_tab, h + 1)
                for n, t in enumerate((cmp, cmp2)):
                    if n:
                        pe.wait_ge(d_tabe, 2 * h + 1)
                    for c in range(TC):
                        last = mm(M0[0:E, c * E:(c + 1) * E], t[:, c, :], ident[0:E, 0:E], start=True, stop=True)
                    last.then_inc(p_tab, 1)

            def slot(t, u, i2, p, groups_behind=2, new=True, nextp=True, one_back=True):
                g = 2 * i2 + p
                two_back = groups_behind > 0 or u > 1
                before_u, before_p = (u - 1) % G, p if u else 1 - p
                if u == 2 and nextp:
                    prep_v(g + 1, 1 - p)
                if new:
                    if u == 0:
                        pe.wait_ge(a_q, g + 1)
                        pe.wait_ge(d_bd, g + 1)
                        pe.wait_ge(a_v, g + 1)
                    scores(t, u, p)
                if two_back:
                    attn_across(t - 2)
                if one_back:
                    probs_across(t - 1, 0)
                    probs_across(t - 1, 1)
                if two_back:
                    project(t - 2)
                if u == 0 and groups_behind > 1:
                    ranks(g - 2)
                if one_back:
                    probs_across(t - 1, 2)
                if u == 1 and nextp:
                    prep_q(g + 1)
                if one_back:
                    weighted_values(t - 1, before_u, before_p, 0)
                    weighted_values(t - 1, before_u, before_p, 1)
                    probs_across(t - 1, 3)
                if u == 2 and groups_behind > 0 and new:
                    normed2_across(g - 1, 1 - p, g + 2 if nextp else NG)
                if one_back:
                    weighted_values(t - 1, before_u, before_p, 2)
                if u == 1 and nextp:
                    prep_k(g + 1, 1 - p, i2 + p)
                if one_back:
                    weighted_values(t - 1, before_u, before_p, 3)
                if u == 0 and nextp:
                    prep_tokens(g + 1)
                if u == 2 and groups_behind > 0 and new:
                    logits(g - 1, 1 - p)

            def step(i2, p, groups_behind=2, last=False, half=False):
                for u in range(G):
                    slot(G * (2 * i2 + p) + u, u, i2, p, groups_behind=groups_behind, nextp=not last,
                         one_back=groups_behind > 0 or u > 0)
                if half:
                    pe.wait_ge(a_es, 2 * i2 + p)
                    table(0)

            pe.wait_ge(s_const, 10)
            pe.wait_ge(s_init, 1)
            pe.wait_ge(s_vinit, 1)
            pe.wait_ge(s_w, 16 * 10)
            prep_tokens(0)
            prep_q(0)
            prep_k(0, 0, 0)
            prep_v(0, 0)
            step(0, 0, groups_behind=0)
            step(0, 1, groups_behind=1)
            with pe.Fori(1, HG // 2) as i2:
                step(i2, 0)
                step(i2, 1)
            step(HG // 2, 0)
            step(HG // 2, 1, half=True)
            with pe.Fori(HG // 2 + 1, NG // 2 - 1) as i2:
                step(i2, 0)
                step(i2, 1)
            step(NG // 2 - 1, 0)
            step(NG // 2 - 1, 1, last=True)
            slot(NT, 0, NG // 2, 0, new=False, nextp=False)
            slot(NT + 1, 1, NG // 2, 0, new=False, nextp=False, one_back=False)
            pe.wait_ge(d_slots, NG - 1)
            normed2_across(NG - 1, 1, NG)
            logits(NG - 1, 1)
            ranks(NG - 1)
            table(1)

            def turn(j, r, round_):
                pe.wait_ge(s_rin[r], 16 * G * round_)
                for u in range(G):
                    last = nc.tensor.transpose(PX[:, u * P:(u + 1) * P], rin[r][:, u, 0:D], ident[:, :])
                last.then_inc(p_bx, 1)

            def gate_up(j):
                ex = read_four(mybir.EngineType.PE, tile_exp, j * G, E - 1)
                pe.wait_ge(a_bx, j + 1)
                wait(pe, d_bh, j)
                for u in range(G):
                    last = mm(banks[:, u // 2, (u % 2) * WGU:(u % 2 + 1) * WGU], b_xt[:, u * P:(u + 1) * P],
                              wgu[:, bass.ds(ex[u], 1), :], start=True, stop=True)
                last.then_inc(p_bgu, 1)

            def down(j):
                ex = read_four(mybir.EngineType.PE, tile_exp, j * G, E - 1)
                pe.wait_ge(a_bht, j + 1)
                wait(pe, d_by, j)
                for u in range(G):
                    last = mm(PY[:, u * D:(u + 1) * D], b_ht[0:I, u * P:(u + 1) * P],
                              wd[:, bass.ds(ex[u], 1), :], start=True, stop=True)
                last.then_inc(p_by, 1)

            def expert_steps(i, last_one=False):
                for q in range(STEPS):
                    j = STEPS * i + q
                    more = not (last_one and q == STEPS - 1)
                    if more:
                        turn(j + 1, (q + 1) % RING, 2 * i + ((q + 1) // RING + 1))
                    pe.wait_ge(d_bh, j + 1)
                    for u in range(G):
                        last = nc.tensor.transpose(PH[0:I, u * P:(u + 1) * P], b_h[:, u * I:(u + 1) * I],
                                                   ident[:, :])
                    last.then_inc(p_bht, 1)
                    if more:
                        gate_up(j + 1)
                    down(j)
                    if q in (2, 5):
                        a = (q - 2) // 3
                        if a == 0:
                            pe.wait_ge(s_shx, 16 * i + 16)
                        toks = sh_x[:, :]
                        mm(SHG[0:I, :], sg_w[:, a * I:(a + 1) * I], toks, start=True, stop=True)
                        mm(SHU[0:I, :], su_w[:, a * I:(a + 1) * I], toks, start=True, stop=True).then_inc(p_shgu, 1)
                    if q == 7:
                        pe.wait_ge(d_shh, 2 * i + 2)
                        for u in range(G):
                            for a in range(2):
                                last = mm(SHO[:, u * D:(u + 1) * D], sh_h[:, a, u * P:(u + 1) * P], sd_w[:, a, :],
                                          start=(a == 0), stop=(a == 1))
                        last.then_inc(p_sho, 1)

            pe.wait_ge(s_wexp, 16 * 6)
            pe.wait_ge(d_tabe, 4)
            turn(0, 0, 1)
            gate_up(0)
            expert_steps(0)
            with pe.Fori(1, NG - 1) as i:
                expert_steps(i)
            expert_steps(NG - 1, last_one=True)


_NAMES = ["x", "ctx_768", "wq", "bq", "wk", "bk", "wv", "bv", "wo", "bo", "gate_w", "gate_bias",
          "Wg", "Wu", "Wd", "Sg", "Su", "Sd"]


def kernel(**inputs):
    import numpy as _np
    import concourse.bacc as _bacc
    from concourse import mybir as _mybir
    from concourse.bass_utils import run_bass_kernel_spmd as _run

    a = {}
    for name in _NAMES:
        full = name if name in inputs else ("L0_xattn_" if "L0_xattn_" + name in inputs else "L0_ffn_") + name
        a[name] = _np.asarray(inputs[full])
    a["ctx_768"] = a["ctx_768"].transpose(2, 0, 1).reshape(DC, NT * SK)
    a["gate_w"] = a["gate_w"].T
    for name in ("Wg", "Wu"):
        a[name] = a[name].transpose(2, 0, 1)
    a["Wd"] = a["Wd"].transpose(2, 0, 1)
    for name in ("Sg", "Su", "Sd"):
        a[name] = a[name].T
    nc = _bacc.Bacc("TRN2", target_bir_lowering=False, num_devices=1)
    arrays, args = {}, []
    for name in _NAMES:
        arr = _np.ascontiguousarray(a[name])
        arrays[f"in_{name}"] = arr
        args.append(nc.dram_tensor(f"in_{name}", arr.shape, _mybir.dt.from_np(arr.dtype), kind="ExternalInput").ap())
    args.append(nc.dram_tensor("out_0", (NT, P, D), _mybir.dt.float32, kind="ExternalOutput").ap())
    moe_block(nc, *args)
    r = _run(nc, [arrays], core_ids=[0])
    return r.results[0]["out_0"]
```

```python
from contextlib import ExitStack

import concourse.bass as bass
from concourse import mybir

F32 = mybir.dt.float32
BF16 = mybir.dt.bfloat16
I32 = mybir.dt.int32
ALU = mybir.AluOpType
ACT = mybir.ActivationFunctionType
X = mybir.AxisListType.X

P = 128
NT = 64
D = 128
DC = 96
SK = 77
NH, DH = 16, 8
SCALE = float(DH) ** -0.5
QH = 4
G = 4
NG = NT // G
E, I = 64, 88
EG = 8
TOPG = 4
K = 8
ROUTED_SCALE = 2.5
EPS = 1e-5
GUESS = float(0x5F3759DF)
HALVES = 2
HG = NG // HALVES
HT = NT * P // HALVES
CAP = HT + P
BT = HT * K // P + E
DUMMY = BT - HT * K // P
XROWS = E * CAP + DUMMY * P
RW = D + K + 1
TOKENS = NT * P
BG = BT // G
STEPS = HALVES * BG // NG
RING = 5
TC = BT // E
WG1 = I + 1
WGU = 2 * I + 1
FAR = 1.0e6
TAKEN = -3.0e38
NOWHERE = 3.0e38


def moe_block(nc, x, ctxt, wq, bq, wk, bk, wv, bv, wo, bo, gatet, gbias, wgt, wut, wdt, sgt, sut, sdt, out):
    ctx = ExitStack()
    with ctx:
        def sb(name, shape, dt=F32):
            return ctx.enter_context(nc.sbuf_tensor(name, shape, dt))

        def sem(name):
            return ctx.enter_context(nc.semaphore(name))

        routed_rows = [nc.dram_tensor(f"routed_rows{h}", [XROWS, RW], F32, kind="Internal").ap()
                       for h in range(HALVES)]
        normed_t = nc.dram_tensor("normed_t", [NG * P, G * P], F32, kind="Internal").ap()
        expert_out = nc.dram_tensor("expert_out", [TOKENS * K, D], F32, kind="Internal").ap()

        wq_sb = sb("wq_sb", [P, D])
        bq_sb = sb("bq_sb", [P, 1])
        bq_scaled = sb("bq_scaled", [P, 1])
        wk_sb = sb("wk_sb", [DC + 1, D])
        wv_sb = sb("wv_sb", [DC + 1, D])
        wo_sb = sb("wo_sb", [P, D])
        bo_sb = sb("bo_sb", [P, D])
        gate_sb = sb("gate_sb", [P, E])
        gbias_sb = sb("gbias_sb", [P, E])
        wgu = sb("wgu", [P, E, WGU])
        wd = sb("wd", [I, E, D])
        sg_w = sb("sg_w", [P, 2 * I])
        su_w = sb("su_w", [P, 2 * I])
        sd_w = sb("sd_w", [I, 2, D])
        ident = sb("ident", [P, P])
        upper = sb("upper", [P, P], BF16)
        ones_bf = sb("ones_bf", [P, P], BF16)
        head_bd = sb("head_bd", [P, NH])
        head_mask = sb("head_mask", [P, QH])
        key_start = sb("key_start", [P, E])
        tok8 = sb("tok8", [P, NT])
        rank8 = sb("rank8", [P, K])
        part1 = sb("part1", [P, 1])
        tile_no = sb("tile_no", [E, TC])
        pad_rows = sb("pad_rows", [P, RW])
        ones_e = sb("ones_e", [P, E])

        xres = sb("xres", [P, NT * D])
        score_sum = sb("score_sum", [P, NT])
        out_scale = sb("out_scale", [P, NT])
        own_key = sb("own_key", [P, HALVES * BT])
        tile_row = sb("tile_row", [1, HALVES * BT], I32)
        tile_exp = sb("tile_exp", [1, HALVES * BT], I32)
        pad_row = sb("pad_row", [1, HALVES * E], I32)

        SCW = NH * SK
        ARENA = 2 * G * P + 2 * G * QH * SK + SCW + NH * P + 2 * G * NH * 32
        arena = sb("arena", [P, ARENA])
        at = [0]

        def carve(width):
            a = arena[:, at[0]:at[0] + width]
            at[0] += width
            assert at[0] <= ARENA
            return a

        q_t = [carve(G * P) for _ in range(2)]
        k_bd = [carve(G * QH * SK) for _ in range(2)]
        probs = carve(SCW)
        probs_t = carve(NH * P)
        v_pad = [carve(G * NH * 32) for _ in range(2)]
        at[0] = 0
        rin_f = [carve(G * RW) for _ in range(RING)]
        rin = [r.rearrange("p (u w) -> p u w", w=RW) for r in rin_f]
        ring_y = [carve(G * D).rearrange("p (u d) -> p u d", d=D) for _ in range(RING)]
        b_xt = carve(G * P)
        b_sig = [carve(G * WG1).rearrange("p (b u w) -> p b u w", b=2, u=2) for _ in range(2)]
        b_h = carve(G * I)
        b_ht = carve(G * P)

        ctx_sb = [sb(f"ctx_sb{i}", [DC + 1, G * SK]) for i in range(2)]
        normed_space = sb("normed_space", [P, 4 * G * P])
        xn, xn_t = normed_space[:, 0:G * D], normed_space[:, G * P:2 * G * P]
        xn2_t = [normed_space[:, (2 + i) * G * P:(3 + i) * G * P] for i in range(2)]
        back_ring = [normed_space[:, r * K * D:(r + 1) * K * D] for r in range(2)]
        stats = sb("stats", [P, 2 * G, 6])
        mv = sb("mv", [P, 2 * G, 2])
        rstd = sb("rstd", [P, 2 * G])
        var_eps = sb("var_eps", [P, 2 * G])
        var_half = sb("var_half", [P, 2 * G])
        guess = sb("guess", [P, 2 * G], I32)
        square = sb("square", [P, 2 * G])
        row_min = sb("row_min", [P, NH])
        den = [sb(f"den{i}", [P, NH]) for i in range(2)]
        rden = sb("rden", [P, NH])
        rden_wide = sb("rden_wide", [P, D])
        ao = sb("ao", [P, D])
        ao_t = sb("ao_t", [P, P])
        denom = sb("denom", [P, P])
        rows = [sb(f"rows{i}", [P, G, RW]) for i in range(2)]
        slots = [sb(f"slots{i}", [P, G, K], I32) for i in range(2)]
        es = sb("es", [P, G, E])
        score = sb("score", [P, G, E])
        choice = sb("choice", [P, G, E])
        masked = sb("masked", [P, G, E])
        taken = sb("taken", [P, G, E])
        tmp = sb("tmp", [P, G, E])
        tmp2 = sb("tmp2", [P, G, E])
        hi4 = sb("hi4", [P, G * EG, 4])
        lo4 = sb("lo4", [P, G * EG, 4])
        hi2 = sb("hi2", [P, G * EG, 2])
        lo2 = sb("lo2", [P, G * EG, 2])
        mid2 = sb("mid2", [P, G * EG, 2])
        hi1 = sb("hi1", [P, G * EG])
        lo1 = sb("lo1", [P, G * EG])
        mid1 = sb("mid1", [P, G * EG])
        gscore = sb("gscore", [P, G, EG])
        gmask = sb("gmask", [P, G, EG])
        gtop = sb("gtop", [P, G, EG])
        gtaken = sb("gtaken", [P, G, EG])
        top8 = sb("top8", [P, G, K])
        chosen = sb("chosen", [P, G, E], BF16)
        base = sb("base", [P, E])
        cnt_i = sb("cnt_i", [P, E], I32)
        n_tiles = sb("n_tiles", [P, E])
        tiles_end = sb("tiles_end", [P, E])
        cmp = sb("cmp", [E, TC, E])
        cmp2 = sb("cmp2", [E, TC, E])
        t_exp = sb("t_exp", [E, TC])
        t_cst = sb("t_cst", [E, TC])
        t_row = sb("t_row", [E, TC])
        idx_ring = [sb(f"idx_ring{r}", [P, G], I32) for r in range(RING)]
        key_eq = sb("key_eq", [P, G, K])
        key_rk = sb("key_rk", [P, G])

        banks = ctx.enter_context(nc.psum_tensor("banks", [P, 8, 512], F32))
        T = [banks[:, 4, :], banks[:, 5, :]]
        M0 = banks[:, 6, :]
        M1 = banks[:, 7, :]
        PV, DENOM, PROJ = M1[:, 0:P], M1[:, P:2 * P], M1[:, 2 * P:3 * P]
        PX, PH, PY = banks[:, 4, :], banks[:, 5, :], banks[:, 2, :]
        PG = banks[:, 0:2, 0:2 * WGU].rearrange("p b (u w) -> p b u w", w=WGU)
        SHG, SHU, SHO = banks[:, 3, :], banks[:, 6, :], banks[:, 7, :]
        sh_x = sb("sh_x", [P, G * P])
        sh_sig = sb("sh_sig", [I, G * P])
        sh_h = sb("sh_h", [I, 2, G * P])

        c_ring = [wgu[:, :, :].rearrange("p e w -> p (e w)")[:, r * K * D:(r + 1) * K * D] for r in range(G)]

        s_x = sem("s_x")
        s_xrest = sem("s_xrest")
        s_w = sem("s_w")
        s_wexp = sem("s_wexp")
        s_ctx = [sem(f"s_ctx{i}") for i in range(2)]
        s_scat = [sem(f"s_scat{i}") for i in range(2)]
        s_pad = sem("s_pad")
        s_norm = [sem(f"s_norm{i}") for i in range(2)]
        s_shx = sem("s_shx")
        s_rin = [sem(f"s_rin{r}") for r in range(RING)]
        s_ysc = [sem(f"s_ysc{r}") for r in range(RING)]
        s_cin = [sem(f"s_cin{r}") for r in range(G)]
        s_back = [sem(f"s_back{r}") for r in range(2)]
        s_out = sem("s_out")
        g_turn = sem("g_turn")
        s_const = sem("s_const")
        s_init = sem("s_init")
        s_vinit = sem("s_vinit")
        p_tr1 = sem("p_tr1")
        p_q = sem("p_q")
        p_k = sem("p_k")
        p_v = sem("p_v")
        p_sc = sem("p_sc")
        p_pt = sem("p_pt")
        p_pv = sem("p_pv")
        p_proj = sem("p_proj")
        p_tr2 = sem("p_tr2")
        p_logit = sem("p_logit")
        p_rank = sem("p_rank")
        p_tab = sem("p_tab")
        p_bx = sem("p_bx")
        p_bgu = sem("p_bgu")
        p_bht = sem("p_bht")
        p_by = sem("p_by")
        p_shgu = sem("p_shgu")
        p_sho = sem("p_sho")
        a_xnt = sem("a_xnt")
        a_q = sem("a_q")
        a_v = sem("a_v")
        a_exp = sem("a_exp")
        a_bd = sem("a_bd")
        a_pt = sem("a_pt")
        a_xn2t = sem("a_xn2t")
        a_es = sem("a_es")
        a_es1 = sem("a_es1")
        a_bx = sem("a_bx")
        a_bht = sem("a_bht")
        a_bsig = sem("a_bsig")
        a_shsig = sem("a_shsig")
        d_xn = sem("d_xn")
        d_sub = sem("d_sub")
        d_rden = sem("d_rden")
        d_ao = sem("d_ao")
        d_res = sem("d_res")
        d_xn2 = sem("d_xn2")
        d_chosen = sem("d_chosen")
        d_slots = sem("d_slots")
        d_tab = sem("d_tab")
        d_tabe = sem("d_tabe")
        d_bh = sem("d_bh")
        d_by = sem("d_by")
        d_shh = sem("d_shh")
        d_sho = sem("d_sho")
        d_fin = sem("d_fin")

        FINISH = (1, 4, 7, 9)
        assert len(FINISH) == G

        def wait(eng, s, value):
            if not (isinstance(value, int) and value <= 0):
                eng.wait_ge(s, value)

        def read_four(eng, words, at, top):
            return nc.values_load_multi_w_load_instructions(
                words[0:1, bass.ds(at, G)], engines=[eng], min_val=0, max_val=top,
                skip_runtime_bounds_check_because="the table is worked out within these bounds")[1]

        def bank_scores(h):
            return banks[:, 2 * h:2 * h + 2, 0:QH * SK].rearrange("p b (j k) -> p b j k", k=SK)

        block = ctx.enter_context(nc.Block())

        @block.sync
        def _(sp):
            x_v = x.rearrange("t p d -> p t d")
            xres_v = xres[:, :].rearrange("p (t d) -> p t d", d=D)
            sp.dma_start(xres_v[:, 0:G, :], x_v[:, 0:G, :]).then_inc(s_x, 16)
            sp.dma_start(wq_sb[:, :], wq).then_inc(s_w, 16)
            sp.dma_start(bq_sb[:, :], bq.rearrange("(p a) -> p a", a=1)).then_inc(s_w, 16)

            def load_ctx(i2, p):
                g = 2 * i2 + p
                wait(sp, p_v, g - 1)
                sp.dma_start(ctx_sb[p][0:DC, :], ctxt[:, bass.ds(g * (G * SK), G * SK)]).then_inc(s_ctx[p], 16)

            load_ctx(0, 0)
            load_ctx(0, 1)
            sp.dma_start(xres_v[:, G:NT, :], x_v[:, G:NT, :]).then_inc(s_xrest, 16)
            sp.wait_ge(s_w, 16 * 10)
            sp.dma_start(wgu[:, :, 0:I], wgt).then_inc(s_wexp, 16)
            sp.dma_start(wgu[:, :, WG1:WGU], wut).then_inc(s_wexp, 16)
            sp.dma_start(wd[:, :, :], wdt).then_inc(s_wexp, 16)
            sp.dma_start(sg_w[:, :], sgt).then_inc(s_wexp, 16)
            sp.dma_start(su_w[:, :], sut).then_inc(s_wexp, 16)
            sp.dma_start(sd_w[:, :, :], sdt.rearrange("(a i) d -> i a d", i=I)).then_inc(s_wexp, 16)
            sp.wait_ge(s_init, 1)
            for h in range(HALVES):
                sp.dma_start(routed_rows[h][E * CAP:XROWS, :].rearrange("(r p) w -> p r w", p=P),
                             pad_rows[:, :].rearrange("p (a w) -> p a w", a=1).to_broadcast([P, DUMMY, RW])
                             ).then_inc(s_pad, 16)

            def pads(h, i):
                ends = read_four(mybir.EngineType.SP, pad_row, i * G + h * E, E * CAP - P)
                for u in range(G):
                    sp.dma_start(routed_rows[h][bass.ds(ends[u], P), :], pad_rows[:, :]).then_inc(s_pad, 16)

            with sp.Fori(1, HG // 2 + 2) as i2:
                load_ctx(i2, 0)
                load_ctx(i2, 1)
            sp.wait_ge(d_tabe, 2)
            with sp.Fori(0, E // G) as i:
                pads(0, i)
            with sp.Fori(HG // 2 + 2, NG // 2) as i2:
                load_ctx(i2, 0)
                load_ctx(i2, 1)

            def load_shared(i):
                wait(sp, p_shgu, 2 * i)
                sp.dma_start(sh_x[:, :], normed_t[bass.ds(i * P, P), :]).then_inc(s_shx, 16)

            def load_rows(h, i, q):
                j = STEPS * i + q
                r = q % RING
                if not (isinstance(i, int) and j < RING):
                    sp.wait_ge(d_by, j - (RING - 1))
                    sp.wait_ge(p_bx, j - (RING - 1))
                first_rows = read_four(mybir.EngineType.SP, tile_row, j * G, XROWS - P)
                for u in range(G):
                    sp.dma_start(rin[r][:, u, :], routed_rows[h][bass.ds(first_rows[u], P), :]
                                 ).then_inc(s_rin[r], 16)

            sp.wait_ge(d_slots, HG + 2)
            sp.wait_ge(s_pad, 16 * (HALVES + E))
            sp.wait_ge(d_res, NT)
            for p in range(2):
                sp.wait_ge(s_norm[p], 16 * NG // 2)
            load_shared(0)
            for q in range(STEPS):
                load_rows(0, 0, q)
            sp.wait_ge(d_tabe, 4)
            pads(1, 0)
            pads(1, 1)
            with sp.Fori(1, NG // 2) as i:
                load_shared(i)
                for q in range(STEPS):
                    load_rows(0, i, q)
                    if q in (2, 7):
                        pads(1, 2 * i + q // 5)
            for p in range(2):
                sp.wait_ge(s_scat[p], 16 * G * K * NG // 2)
            sp.wait_ge(s_pad, 16 * (HALVES + 2 * E))
            back = expert_out.rearrange("(n k) d -> n (k d)", k=K)

            def load_first_back(i, m):
                n = (i - NG // 2) * G + m
                for r in range(RING):
                    sp.wait_ge(s_ysc[r], 16 * G * BG // RING)
                wait(sp, d_fin, n - 1)
                sp.dma_start(back_ring[m % 2], back[bass.ds(n * P, P), :]).then_inc(s_back[m % 2], 16)

            def second_round(i):
                load_shared(i)
                for q in range(STEPS):
                    load_rows(1, i, q)
                    if q in FINISH:
                        load_first_back(i, FINISH.index(q))

            second_round(NG // 2)
            with sp.Fori(NG // 2 + 1, NG) as i:
                second_round(i)

            for r in range(RING):
                sp.wait_ge(s_ysc[r], 16 * G * HALVES * BG // RING)

            def load_back(i, r):
                if not isinstance(i, int):
                    sp.wait_ge(d_fin, i * G + (r + 1 - G))
                sp.dma_start(c_ring[r], back[bass.ds((i * G + r) * P, P), :]).then_inc(s_cin[r], 16)

            for r in range(G):
                load_back(NG // 2, r)
            with sp.Fori(NG // 2 + 1, NG) as i:
                for r in range(G):
                    load_back(i, r)
            sp.wait_ge(s_out, 16 * NG)

        @block.gpsimd
        def _(pool):
            nc.gpsimd.memset(ident[:, :], 0.0).then_inc(s_const, 1)
            nc.gpsimd.memset(upper[:, :], 1.0).then_inc(s_const, 1)
            nc.gpsimd.memset(head_bd[:, :], -1.0).then_inc(s_const, 1)
            pool.wait_ge(s_const, 3)
            nc.gpsimd.affine_select(out=ident[:, :], in_=ident[:, :], compare_op=ALU.not_equal, fill=1.0,
                                    base=0, pattern=[[-1, P]], channel_multiplier=1).then_inc(s_const, 1)
            nc.gpsimd.affine_select(out=upper[:, :], in_=upper[:, :], compare_op=ALU.is_gt, fill=0.0,
                                    base=0, pattern=[[1, P]], channel_multiplier=-1).then_inc(s_const, 1)
            nc.gpsimd.affine_select(out=head_bd[:, :], in_=head_bd[:, :], compare_op=ALU.is_ge, fill=0.0,
                                    base=0, pattern=[[-DH, NH]], channel_multiplier=1).then_inc(s_const, 1)
            pool.wait_ge(s_const, 6)
            nc.gpsimd.affine_select(out=head_bd[:, :], in_=head_bd[:, :], compare_op=ALU.is_ge, fill=0.0,
                                    base=DH - 1, pattern=[[DH, NH]], channel_multiplier=-1).then_inc(s_const, 1)
            imprecise = dict(allow_small_or_imprecise_dtypes=True)
            nc.gpsimd.iota(key_start[:, :], [[CAP, E]], base=1, channel_multiplier=0, **imprecise)
            nc.gpsimd.iota(tok8[:, :], [[P * K, NT]], base=0, channel_multiplier=K, **imprecise)
            nc.gpsimd.iota(rank8[:, :], [[1, K]], base=0, channel_multiplier=0, **imprecise)
            nc.gpsimd.iota(part1[:, :], [[0, 1]], base=1, channel_multiplier=1, **imprecise)
            nc.gpsimd.iota(tile_no[:, :], [[E, TC]], base=0, channel_multiplier=1, **imprecise).then_inc(s_const, 1)

            def scatter(h, i2, p):
                pool.wait_ge(d_slots, 2 * i2 + (p + 1))
                pool.sem_inc(g_turn, 1)
                for u in range(G):
                    for k in range(K):
                        nc.gpsimd.indirect_dma_start(
                            out=routed_rows[h], out_offset=bass.IndirectOffsetOnAxis(ap=slots[p][:, u, k:k + 1], axis=0),
                            in_=rows[p][:, u, :], in_offset=None).then_inc(s_scat[p], 16)

            for h in range(HALVES):
                with pool.Fori(h * HG // 2, (h + 1) * HG // 2) as i2:
                    scatter(h, i2, 0)
                    scatter(h, i2, 1)
            with pool.Fori(0, NG) as i:
                for q in range(STEPS):
                    r = q % RING
                    pool.wait_ge(d_by, STEPS * i + (q + 1))
                    pool.sem_inc(g_turn, 1)
                    for u in range(G):
                        nc.gpsimd.indirect_dma_start(
                            out=expert_out, out_offset=bass.IndirectOffsetOnAxis(ap=idx_ring[r][:, u:u + 1], axis=0),
                            in_=ring_y[r][:, u, :], in_offset=None, bounds_check=TOKENS * K - 1,
                            oob_is_err=False).then_inc(s_ysc[r], 16)

        @block.scalar
        def _(act):
            act.dma_start(wk_sb[0:DC, :], wk).then_inc(s_w, 16)
            act.dma_start(wk_sb[DC:DC + 1, :], bk.rearrange("(a n) -> a n", a=1)).then_inc(s_w, 16)
            act.dma_start(wv_sb[0:DC, :], wv).then_inc(s_w, 16)
            act.dma_start(wv_sb[DC:DC + 1, :], bv.rearrange("(a n) -> a n", a=1)).then_inc(s_w, 16)
            act.dma_start(wo_sb[:, :], wo).then_inc(s_w, 16)
            act.dma_start(bo_sb[:, :], bo.rearrange("(a n) -> a n", a=1).to_broadcast([P, D])).then_inc(s_w, 16)
            act.dma_start(gate_sb[:, :], gatet).then_inc(s_w, 16)
            act.dma_start(gbias_sb[:, :], gbias.rearrange("(a n) -> a n", a=1).to_broadcast([P, E])).then_inc(s_w, 16)
            def normed_out(gp):
                act.wait_ge(p_tr1, gp + 1)
                nc.scalar.activation(xn_t[:, :], T[0], ACT.Copy).then_inc(a_xnt, 1)

            def query_out(gp, p):
                if isinstance(gp, int) and gp == 0:
                    act.wait_ge(s_vinit, 2)
                act.wait_ge(p_q, gp + 1)
                nc.scalar.activation(q_t[p], M0, ACT.Identity, bias=bq_scaled[:, 0:1],
                                     scale=SCALE).then_inc(a_q, 1)

            def value_out(gp, p):
                act.wait_ge(p_v, gp + 1)
                if isinstance(gp, int) and gp < 2:
                    act.wait_ge(s_vinit, 1)
                dst = v_pad[p][0:SK, :].rearrange("k (a w) -> k a w", w=QH * 32)
                src = M0[0:SK, :].rearrange("k (a j c) -> k a j c", j=QH, c=DH)
                for j in range(QH):
                    last = nc.scalar.activation(dst[:, :, 40 * j:40 * j + DH], src[:, :, j, :], ACT.Copy)
                last.then_inc(a_v, 1)

            def probs_out(t, i):
                act.wait_ge(p_pt, 4 * t + (i + 1))
                nc.scalar.activation(probs_t[0:SK, i * 512:(i + 1) * 512], T[i % 2][0:SK, :],
                                     ACT.Copy).then_inc(a_pt, 1)

            def exp(t, u, h):
                act.wait_ge(d_sub, 2 * t + (h + 1))
                for n in range(h * NH // 2, (h + 1) * NH // 2):
                    last = nc.scalar.activation(probs[:, n * SK:(n + 1) * SK],
                                                banks[:, n // QH, n % QH * SK:(n % QH + 1) * SK], ACT.Exp,
                                                scale=-1.0, bias=row_min[:, n:n + 1],
                                                accum_out=den[u % 2][:, n:n + 1])
                last.then_inc(a_exp, 1)

            def keys_out(gp, p):
                act.wait_ge(p_k, gp + 1)
                if isinstance(gp, int) and gp < 2:
                    act.wait_ge(s_vinit, 1)
                k_v = k_bd[p].rearrange("p (u j k) -> p u j k", u=G, j=QH)
                src = M0[:, 0:G * SK].rearrange("p (u k) -> p u k", k=SK)
                for j in range(QH):
                    last = nc.scalar.activation(k_v[:, :, j, :], src, ACT.Copy, scale=head_mask[:, j:j + 1])
                last.then_inc(a_bd, 1)

            def normed2_out(g, i2, p):
                act.wait_ge(p_tr2, g + 1)
                wait(act, s_norm[p], 16 * i2)
                nc.scalar.activation(xn2_t[p][:, :], T[0], ACT.Copy).then_inc(a_xn2t, 1)

            def logits_out(g, p):
                act.wait_ge(p_logit, g + 1)
                nc.scalar.activation(es[:, :, :], M0[:, 0:G * E].rearrange("p (u e) -> p u e", e=E), ACT.Exp,
                                     scale=-1.0).then_inc(a_es, 1)
                act.wait_ge(a_es, g + 1)
                nc.scalar.activation(tmp[:, :, :], es[:, :, :], ACT.Copy, bias=1.0).then_inc(a_es1, 1)
                act.wait_ge(a_xn2t, g + 1)
                act.dma_start(normed_t[bass.ds(g * P, P), :], xn2_t[p][:, :]).then_inc(s_norm[p], 16)

            def slot(t, u, g, i2, p, one_back=True, scores=True, nextp=True, route=True):
                if u == 1 and nextp:
                    normed_out(g + 1)
                if u == 2 and route:
                    normed2_out(g - 1, i2 - 1 + p, 1 - p)
                if one_back:
                    for i in range(4):
                        probs_out(t - 1, i)
                if u == 1 and nextp:
                    query_out(g + 1, 1 - p)
                if u == 2 and route:
                    logits_out(g - 1, 1 - p)
                if scores:
                    exp(t, u, 0)
                    exp(t, u, 1)
                if u == 1 and nextp:
                    keys_out(g + 1, 1 - p)
                if u == 2 and nextp:
                    value_out(g + 1, 1 - p)

            def step(i2, p, first=False, last=False):
                g = 2 * i2 + p
                for u in range(G):
                    slot(G * g + u, u, g, i2, p, one_back=not first or u > 0, nextp=not last, route=not first)

            normed_out(0)
            query_out(0, 0)
            keys_out(0, 0)
            value_out(0, 0)
            step(0, 0, first=True)
            step(0, 1)
            step(1, 0)
            step(1, 1)
            with act.Fori(2, NG // 2 - 1) as i2:
                step(i2, 0)
                step(i2, 1)
            step(NG // 2 - 1, 0)
            step(NG // 2 - 1, 1, last=True)
            slot(NT, 0, NG, NG // 2, 0, scores=False, nextp=False)
            normed2_out(NG - 1, NG // 2 - 1, 1)
            logits_out(NG - 1, 1)

            def front(j, p):
                act.wait_ge(p_bx, j + 1)
                nc.scalar.activation(b_xt, PX, ACT.Copy).then_inc(a_bx, 1)
                act.wait_ge(p_bgu, j + 1)
                nc.scalar.activation(b_sig[p], PG[:, :, :, 0:WG1], ACT.Sigmoid).then_inc(a_bsig, 1)

            def expert_steps(i, last=False):
                for q in range(STEPS):
                    j = STEPS * i + q
                    more = not (last and q == STEPS - 1)
                    if more:
                        act.wait_ge(p_bx, j + 2)
                        nc.scalar.activation(b_xt, PX, ACT.Copy).then_inc(a_bx, 1)
                    act.wait_ge(p_bht, j + 1)
                    nc.scalar.activation(b_ht[0:I, :], PH[0:I, :], ACT.Copy).then_inc(a_bht, 1)
                    if more:
                        act.wait_ge(p_bgu, j + 2)
                        wait(act, d_by, j)
                        nc.scalar.activation(b_sig[(q + 1) % 2], PG[:, :, :, 0:WG1], ACT.Sigmoid).then_inc(a_bsig, 1)
                    if q in (3, 6):
                        a = (q - 3) // 3
                        act.wait_ge(p_shgu, 2 * i + (a + 1))
                        nc.scalar.activation(sh_sig[:, :], SHG[0:I, :], ACT.Sigmoid).then_inc(a_shsig, 1)

            def store(i):
                act.wait_ge(d_fin, G * i + G)
                act.dma_start(out[bass.ds(i * G, G), :, :].rearrange("t p d -> p t d"),
                              xres[:, bass.ds(i * (G * D), G * D)].rearrange("p (t d) -> p t d", d=D)
                              ).then_inc(s_out, 16)

            front(0, 0)
            expert_steps(0)
            with act.Fori(1, NG // 2 + 1) as i:
                expert_steps(i)
            with act.Fori(NG // 2 + 1, NG - 1) as i:
                expert_steps(i)
                store(i - (NG // 2 + 1))
            expert_steps(NG - 1, last=True)
            with act.Fori(NG // 2 - 2, NG) as i:
                store(i)
            act.wait_ge(s_out, 16 * NG)

        @block.vector
        def _(dve):
            v = nc.vector

            def drain():
                dve.drain()

            def norms(tasks):
                n = G * len(tasks)
                for k, (src_group, _, _) in enumerate(tasks):
                    for u in range(G):
                        v.bn_stats(stats[:, k * G + u, :], xres[:, bass.ds(src_group * (G * D) + u * D, D)])
                drain()
                for u in range(n):
                    v.bn_aggr(mv[:, u, :], stats[:, u, :])
                drain()
                v.tensor_scalar(var_eps[:, 0:n], mv[:, 0:n, 1], EPS, None, ALU.add)
                v.tensor_scalar(var_half[:, 0:n], mv[:, 0:n, 1], -0.5, -0.5 * EPS, ALU.mult, ALU.add)
                drain()
                v.tensor_scalar(guess[:, 0:n], var_eps[:, 0:n].bitcast(I32), 1, None, ALU.arith_shift_right)
                drain()
                r = rstd[:, 0:n]
                sq = square[:, 0:n]
                v.tensor_scalar(r.bitcast(I32), guess[:, 0:n], -1.0, GUESS, ALU.mult, ALU.add)
                drain()
                for _ in range(3):
                    v.tensor_tensor(sq, r, r, ALU.mult)
                    drain()
                    v.tensor_tensor(sq, sq, var_half[:, 0:n], ALU.mult)
                    drain()
                    v.scalar_tensor_tensor(out=r, in0=sq, scalar=1.5, in1=r, op0=ALU.add, op1=ALU.mult)
                    drain()
                for k, (src_group, dst, ready) in enumerate(tasks):
                    for u in range(G):
                        last = v.tensor_scalar(dst(u), xres[:, bass.ds(src_group * (G * D) + u * D, D)],
                                               mv[:, k * G + u, 0:1], rstd[:, k * G + u:k * G + u + 1],
                                               ALU.subtract, ALU.mult)
                    last.then_inc(ready, 1)

            def output_bias(g):
                drain()
                xg = xres[:, bass.ds(g * (G * D), G * D)].rearrange("p (u d) -> p u d", d=D)
                v.tensor_tensor(xg, xg, bo_sb[:, :].rearrange("p (a d) -> p a d", a=1).to_broadcast([P, G, D]),
                                ALU.add)

            def prep_norm(gp):
                wait(dve, p_tr1, gp)
                return (gp, lambda u: xn[:, u * D:(u + 1) * D], d_xn)

            def route_norm(g, i2, p):
                wait(dve, s_scat[p], 16 * G * K * i2)
                v.tensor_copy(rows[p][:, :, D + K], tok8[:, bass.ds(g * G, G)])
                return (g, lambda u: rows[p][:, u, 0:D], d_xn2)

            def least(t, h):
                dve.wait_ge(p_sc, 2 * t + (h + 1))
                v.tensor_reduce(row_min[:, h * NH // 2:(h + 1) * NH // 2].rearrange("p (b j) -> p b j", j=QH),
                                bank_scores(h), X, ALU.min).then_inc(d_sub, 1)

            def denominators(t, u):
                dve.wait_ge(a_exp, 2 * t + 2)
                v.reciprocal(rden[:, :], den[u % 2][:, :])
                drain()
                wait(dve, p_pv, t)
                v.tensor_copy(rden_wide[:, :].rearrange("p (n c) -> p n c", c=DH),
                              rden[:, :].rearrange("p (n a) -> p n a", a=1).to_broadcast([P, NH, DH])
                              ).then_inc(d_rden, 1)

            def attn_norm(t):
                dve.wait_ge(p_pv, t + 1)
                v.tensor_copy(denom[:, :], DENOM)
                drain()
                v.tensor_tensor(ao_t[:, :], PV, denom[:, :], ALU.mult).then_inc(d_ao, 1)

            def residual(t):
                dve.wait_ge(p_proj, t + 1)
                xt = xres[:, bass.ds(t * D, D)]
                v.tensor_tensor(xt, PROJ, xt, ALU.add).then_inc(d_res, 1)

            def route_groups(g):
                dve.wait_ge(a_es1, g + 1)
                v.reciprocal(score[:, :, :], tmp[:, :, :])
                drain()
                v.tensor_tensor(choice[:, :, :], score[:, :, :],
                                gbias_sb[:, :].rearrange("p (a e) -> p a e", a=1).to_broadcast([P, G, E]), ALU.add)
                drain()
                cg = choice[:, :, :].rearrange("p u (g k) -> p (u g) k", k=EG)
                v.tensor_tensor(hi4[:, :, :], cg[:, :, 0:4], cg[:, :, 4:8], ALU.max)
                v.tensor_tensor(lo4[:, :, :], cg[:, :, 0:4], cg[:, :, 4:8], ALU.min)
                drain()
                v.tensor_tensor(hi2[:, :, :], hi4[:, :, 0:2], hi4[:, :, 2:4], ALU.max)
                v.tensor_tensor(mid2[:, :, :], hi4[:, :, 0:2], hi4[:, :, 2:4], ALU.min)
                v.tensor_tensor(lo2[:, :, :], lo4[:, :, 0:2], lo4[:, :, 2:4], ALU.max)
                drain()
                v.tensor_tensor(lo2[:, :, :], lo2[:, :, :], mid2[:, :, :], ALU.max)
                v.tensor_tensor(hi1[:, :], hi2[:, :, 0], hi2[:, :, 1], ALU.max)
                v.tensor_tensor(mid1[:, :], hi2[:, :, 0], hi2[:, :, 1], ALU.min)
                drain()
                v.tensor_tensor(lo1[:, :], lo2[:, :, 0], lo2[:, :, 1], ALU.max)
                drain()
                v.tensor_tensor(lo1[:, :], lo1[:, :], mid1[:, :], ALU.max)
                drain()
                v.tensor_tensor(gscore[:, :, :].rearrange("p u g -> p (u g)"), hi1[:, :], lo1[:, :], ALU.add)
                drain()
            def route_masked(g):
                for u in range(G):
                    v.max(gtop[:, u, :], gscore[:, u, :])
                drain()
                v.memset(gtop[:, :, TOPG:], NOWHERE)
                drain()
                for u in range(G):
                    v.match_replace(out=gtaken[:, u, :], in_to_replace=gtop[:, u, :], in_values=gscore[:, u, :],
                                    imm_value=TAKEN)
                drain()
                v.tensor_scalar(gmask[:, :, :], gtaken[:, :, :], TAKEN / 2, None, ALU.is_lt)
                drain()
                cg = choice[:, :, :].rearrange("p u (g k) -> p (u g) k", k=EG)
                v.tensor_tensor(masked[:, :, :].rearrange("p u (g k) -> p (u g) k", k=EG), cg,
                                gmask[:, :, :].rearrange("p u (g a) -> p (u g) a", a=1).to_broadcast([P, G * EG, EG]),
                                ALU.mult)
                drain()

            def route_top(g):
                for u in range(G):
                    v.max(top8[:, u, :], masked[:, u, :])
                drain()
                for u in range(G):
                    v.match_replace(out=taken[:, u, :], in_to_replace=top8[:, u, :], in_values=masked[:, u, :],
                                    imm_value=TAKEN)
                drain()
                v.tensor_scalar(chosen[:, :, :], taken[:, :, :], TAKEN / 2, None, ALU.is_lt).then_inc(d_chosen, 1)
                drain()

            def route_sum(g):
                v.tensor_tensor(tmp[:, :, :], score[:, :, :], chosen[:, :, :], ALU.mult)
                drain()
                v.tensor_reduce(score_sum[:, bass.ds(g * G, G)], tmp[:, :, :], X, ALU.add)

            def route_slots(g, p):
                dve.wait_ge(p_rank, g + 1)
                rk = M0[:, 0:G * E].rearrange("p (u e) -> p u e", e=E)
                v.tensor_tensor(tmp2[:, :, :], rk,
                                base[:, :].rearrange("p (a e) -> p a e", a=1).to_broadcast([P, G, E]), ALU.add)
                drain()
                v.tensor_tensor(base[:, :], M0[:, G * E:G * E + E], base[:, :], ALU.add)
                v.tensor_tensor(tmp2[:, :, :], tmp2[:, :, :], chosen[:, :, :], ALU.mult)
                drain()
                for u in range(G):
                    v.max(rows[p][:, u, D:D + K], tmp2[:, u, :])
                drain()
                v.tensor_scalar(slots[p][:, :, :], rows[p][:, :, D:D + K], -1.0, None,
                                ALU.add).then_inc(d_slots, 1)

            def table(h):
                v.tensor_scalar(pad_row[0:1, h * E:(h + 1) * E], base[0:1, :], -1.0, None, ALU.add)
                v.tensor_tensor(n_tiles[:, :], base[:, :], key_start[:, :], ALU.subtract)
                drain()
                v.tensor_scalar(cnt_i[:, :], n_tiles[:, :], float(P - 1), None, ALU.add)
                drain()
                v.tensor_scalar(cnt_i[:, :], cnt_i[:, :], P.bit_length() - 1, None, ALU.arith_shift_right)
                v.tensor_copy(base[:, :], key_start[:, :])
                drain()
                v.tensor_copy(n_tiles[:, :], cnt_i[:, :])
                drain()
                v.tensor_tensor_scan(tiles_end[:, :], ones_e[:, :], n_tiles[:, :], 0.0, ALU.mult, ALU.add)
                drain()
                shape = [E, TC, E]
                v.tensor_tensor(cmp[:, :, :],
                                tiles_end[0:E, :].rearrange("p (a e) -> p a e", a=1).to_broadcast(shape),
                                tile_no[:, :].rearrange("p (c a) -> p c a", a=1).to_broadcast(shape), ALU.is_le)
                drain()
                v.tensor_reduce(t_exp[:, :], cmp[:, :, :], X, ALU.add)
                v.tensor_tensor(cmp2[:, :, :], cmp[:, :, :],
                                n_tiles[0:E, :].rearrange("p (a e) -> p a e", a=1).to_broadcast(shape), ALU.mult)
                drain()
                v.tensor_reduce(t_cst[:, :], cmp2[:, :, :], X, ALU.add)
                drain()
                v.tensor_tensor(t_cst[:, :], tile_no[:, :], t_cst[:, :], ALU.subtract)
                v.tensor_scalar(t_row[:, :], t_exp[:, :], float(CAP), None, ALU.mult)
                drain()
                v.scalar_tensor_tensor(out=t_row[:, :], in0=t_cst[:, :], scalar=float(P), in1=t_row[:, :],
                                       op0=ALU.mult, op1=ALU.add)
                v.tensor_scalar(t_exp[:, :], t_exp[:, :], float(E - 1), None, ALU.min)
                drain()
                for c in range(TC):
                    v.tensor_copy(cmp[:, c, :], t_row[:, c:c + 1].to_broadcast([E, E]))
                    last = v.tensor_copy(cmp2[:, c, :], t_exp[:, c:c + 1].to_broadcast([E, E]))
                last.then_inc(d_tab, 1)
                dve.wait_ge(p_tab, 2 * h + 1)
                span = slice(h * BT, (h + 1) * BT)
                v.tensor_scalar(own_key[0:E, span], M0[0:E, 0:BT], part1[0:E, 0:1], None, ALU.add)
                v.tensor_scalar(own_key[E:P, span], M0[0:E, 0:BT], part1[E:P, 0:1], None, ALU.add)
                v.tensor_copy(tile_row[0:1, span], M0[0:1, 0:BT]).then_inc(d_tabe, 1)
                dve.wait_ge(p_tab, 2 * h + 2)
                v.tensor_copy(tile_exp[0:1, span], M0[0:1, 0:BT]).then_inc(d_tabe, 1)

            def step(i2, p, groups_behind=2, last=False, half=False, more_norm=True):
                g = 2 * i2 + p
                for u in range(G):
                    t = G * g + u
                    two_back = groups_behind > 0 or u > 1
                    if two_back:
                        attn_norm(t - 2)
                    least(t, 0)
                    if groups_behind > 0 or u > 0:
                        denominators(t - 1, (u - 1) % G)
                    if two_back:
                        residual(t - 2)
                    least(t, 1)
                    if u == 0 and groups_behind > 1:
                        route_slots(g - 2, p)
                        route_sum(g - 2)
                    if u == 1:
                        drain()
                        norms(([route_norm(g - 1, i2 - 1 + p, 1 - p)] if groups_behind > 0 else [])
                              + ([prep_norm(g + 2)] if more_norm else []))
                        if more_norm:
                            output_bias(g + 2)
                    if u == 2 and groups_behind > 0:
                        route_groups(g - 1)
                    if u == 3 and groups_behind > 0:
                        route_masked(g - 1)
                        route_top(g - 1)
                if half:
                    table(0)

            v.memset(ones_bf[:, :], 1.0)
            v.memset(ones_e[:, :], 1.0)
            v.memset(pad_rows[:, 0:D + K], 0.0)
            v.memset(pad_rows[:, D + K:RW], FAR).then_inc(s_init, 1)
            for c in ctx_sb:
                v.memset(c[DC:DC + 1, :], 1.0)
            for c in v_pad:
                v.memset(c[0:SK, :], 0.0)
            dve.wait_ge(s_const, 8)
            v.tensor_reduce(head_mask[:, :], head_bd[:, :].rearrange("p (i j) -> p j i", j=QH), X,
                            ALU.add).then_inc(s_vinit, 1)
            v.tensor_copy(base[:, :], key_start[:, :])
            drain()
            dve.wait_ge(s_x, 16)
            dve.wait_ge(s_w, 16 * 10)
            v.tensor_scalar(bq_scaled[:, :], bq_sb[:, :], SCALE, None, ALU.mult).then_inc(s_vinit, 1)
            norms([prep_norm(0)])
            output_bias(0)
            dve.wait_ge(s_xrest, 16)
            norms([prep_norm(1)])
            output_bias(1)
            dve.wait_ge(s_w, 16 * 10)
            v.tensor_copy(wgu[:, :, I], gate_sb[:, :])
            step(0, 0, groups_behind=0)
            step(0, 1, groups_behind=1)
            step(1, 0)
            step(1, 1)
            with dve.Fori(2, HG // 2) as i2:
                step(i2, 0)
                step(i2, 1)
            step(HG // 2, 0)
            step(HG // 2, 1, half=True)
            with dve.Fori(HG // 2 + 1, NG // 2 - 1) as i2:
                step(i2, 0)
                step(i2, 1)
            step(NG // 2 - 1, 0, more_norm=False)
            step(NG // 2 - 1, 1, last=True, more_norm=False)
            attn_norm(NT - 2)
            denominators(NT - 1, G - 1)
            residual(NT - 2)
            route_slots(NG - 2, 0)
            route_sum(NG - 2)
            attn_norm(NT - 1)
            residual(NT - 1)
            drain()
            norms([route_norm(NG - 1, NG // 2 - 1, 1)])
            route_groups(NG - 1)
            route_masked(NG - 1)
            route_top(NG - 1)
            route_slots(NG - 1, 1)
            route_sum(NG - 1)
            table(1)

            v.tensor_scalar(out_scale[:, :], score_sum[:, :], 1e-20, None, ALU.add)
            drain()
            v.reciprocal(out_scale[:, :], out_scale[:, :])
            drain()
            v.tensor_scalar(out_scale[:, :], out_scale[:, :], ROUTED_SCALE, None, ALU.mult)
            drain()

            h_v = b_h.rearrange("p (b u w) -> p b u w", b=2, u=2)

            def inner(j, p):
                dve.wait_ge(a_bsig, j + 1)
                v.tensor_tensor(h_v, b_sig[p][:, :, :, 0:I], PG[:, :, :, 0:I], ALU.mult)
                drain()
                v.tensor_tensor(h_v, h_v, PG[:, :, :, WG1:WGU], ALU.mult).then_inc(d_bh, 1)

            def places(i, q):
                j = STEPS * i + q
                r = q % RING
                dve.wait_ge(s_rin[r], 16 * G * (2 * i + (q // RING + 1)))
                if not (isinstance(i, int) and j < RING):
                    dve.wait_ge(s_ysc[r], 16 * G * (2 * i + q // RING))
                own = own_key[:, bass.ds(j * G, G)].rearrange("p (u a) -> p u a", a=1).to_broadcast([P, G, K])
                v.tensor_tensor(key_eq[:, :, :], rin[r][:, :, D:D + K], own, ALU.is_equal)
                drain()
                v.tensor_tensor(key_eq[:, :, :], key_eq[:, :, :],
                                rank8[:, :].rearrange("p (a k) -> p a k", a=1).to_broadcast([P, G, K]), ALU.mult)
                drain()
                v.tensor_reduce(key_rk[:, :], key_eq[:, :, :], X, ALU.add)
                drain()
                v.tensor_tensor(idx_ring[r][:, :], key_rk[:, :], rin[r][:, :, D + K], ALU.add)

            def scaled(i, q):
                j = STEPS * i + q
                dve.wait_ge(p_by, j + 1)
                sc = b_sig[q % 2].rearrange("p b u w -> p (b u) w")[:, :, I:WG1].to_broadcast([P, G, D])
                v.tensor_tensor(ring_y[q % RING], PY.rearrange("p (u d) -> p u d", d=D), sc,
                                ALU.mult).then_inc(d_by, 1)

            def finish(n, rows8):
                v.tensor_reduce(ao[:, :], rows8.rearrange("p (k d) -> p d k", k=K), X, ALU.add)
                drain()
                xt = xres[:, bass.ds(n * D, D)]
                v.scalar_tensor_tensor(out=xt, in0=ao[:, :], scalar=out_scale[:, bass.ds(n, 1)], in1=xt,
                                       op0=ALU.mult, op1=ALU.add).then_inc(d_fin, 1)

            def expert_steps(i, last=False, second=False):
                for q in range(STEPS):
                    places(i, q)
                    if not (last and q == STEPS - 1):
                        inner(STEPS * i + (q + 1), (q + 1) % 2)
                    scaled(i, q)
                    if q in (3, 6):
                        a = (q - 3) // 3
                        dve.wait_ge(a_shsig, 2 * i + (a + 1))
                        v.tensor_tensor(sh_h[:, a, :], sh_sig[:, :], SHG[0:I, :], ALU.mult)
                        drain()
                        v.tensor_tensor(sh_h[:, a, :], sh_h[:, a, :], SHU[0:I, :], ALU.mult).then_inc(d_shh, 1)
                    if q == 8:
                        dve.wait_ge(p_sho, i + 1)
                        xt = xres[:, bass.ds(i * (G * D), G * D)]
                        v.tensor_tensor(xt, SHO, xt, ALU.add).then_inc(d_sho, 1)
                    if second and q in FINISH:
                        m = FINISH.index(q)
                        dve.wait_ge(s_back[m % 2], 16 * (2 * (i - NG // 2) + m // 2 + 1))
                        finish((i - NG // 2) * G + m, back_ring[m % 2])

            inner(0, 0)
            expert_steps(0)
            with dve.Fori(1, NG // 2) as i:
                expert_steps(i)
            with dve.Fori(NG // 2, NG - 1) as i:
                expert_steps(i, second=True)
            expert_steps(NG - 1, last=True, second=True)
            drain()

            with dve.Fori(NG // 2, NG) as i:
                for r in range(G):
                    dve.wait_ge(s_cin[r], (i - (NG // 2 - 1)) * 16)
                    finish(i * G + r, c_ring[r])
                    drain()

        @block.tensor
        def _(pe):
            mm = nc.tensor.matmul

            def prep_tokens(gp):
                pe.wait_ge(d_xn, gp + 1)
                for u in range(G):
                    last = nc.tensor.transpose(T[0][:, u * P:(u + 1) * P], xn[:, u * D:(u + 1) * D], ident[:, :])
                last.then_inc(p_tr1, 1)

            def prep_q(gp):
                pe.wait_ge(a_xnt, gp + 1)
                if not isinstance(gp, int) or gp > 2:
                    pe.wait_ge(d_slots, gp - 2)
                mm(M0, wq_sb[:, :], xn_t[:, :], start=True, stop=True).then_inc(p_q, 1)

            def prep_k(gp, p, i2):
                pe.wait_ge(a_q, gp + 1)
                pe.wait_ge(s_ctx[p], 16 * i2 + 16)
                mm(M0[:, 0:G * SK], wk_sb[:, :], ctx_sb[p][:, :], start=True, stop=True).then_inc(p_k, 1)

            def prep_v(gp, p):
                pe.wait_ge(a_bd, gp + 1)
                for u in range(G):
                    last = mm(M0[0:SK, u * D:(u + 1) * D], ctx_sb[p][:, u * SK:(u + 1) * SK], wv_sb[:, :],
                              start=True, stop=True)
                last.then_inc(p_v, 1)

            def scores(t, u, p, h):
                wait(pe, a_exp, 2 * t + (h - 1))
                for b in range(2 * h, 2 * h + 2):
                    rws = slice(32 * b, 32 * b + 32)
                    last = mm(banks[:, b, 0:QH * SK], q_t[p][rws, u * P:(u + 1) * P],
                              k_bd[p][rws, u * QH * SK:(u + 1) * QH * SK], start=True, stop=True)
                last.then_inc(p_sc, 1)

            def probs_across(t, i):
                if i % 2 == 0:
                    pe.wait_ge(a_exp, 2 * t + (i // 2 + 1))
                wait(pe, a_pt, 4 * t + (i - 1))
                for j in range(4):
                    n = 4 * i + j
                    last = nc.tensor.transpose(T[i % 2][0:SK, j * P:(j + 1) * P],
                                               probs[:, n * SK:(n + 1) * SK], ident[:, :])
                last.then_inc(p_pt, 1)

            def weighted_values(t, u, p):
                wait(pe, d_res, t)
                pe.wait_ge(d_rden, t + 1)
                nc.tensor.transpose(DENOM, rden_wide[:, :], ident[:, :])
                pe.wait_ge(a_pt, 4 * t + 4)
                for j in range(QH):
                    for c in range(4):
                        n = QH * c + j
                        last = mm(PV[32 * c:32 * c + 32, :],
                                  v_pad[p][0:SK, (u * NH + n) * 32:(u * NH + n + 1) * 32],
                                  probs_t[0:SK, n * P:(n + 1) * P], start=(j == 0), stop=(j == QH - 1))
                last.then_inc(p_pv, 1)

            def project(t):
                pe.wait_ge(d_ao, t + 1)
                mm(PROJ, ao_t[:, :], wo_sb[:, :], start=True, stop=True).then_inc(p_proj, 1)

            def normed2_across(g, p):
                pe.wait_ge(d_xn2, g + 1)
                for u in range(G):
                    last = nc.tensor.transpose(T[0][:, u * P:(u + 1) * P], rows[p][:, u, 0:D], ident[:, :])
                last.then_inc(p_tr2, 1)

            def logits(g, p):
                pe.wait_ge(a_xn2t, g + 1)
                for u in range(G):
                    last = mm(M0[:, u * E:(u + 1) * E], xn2_t[p][:, u * P:(u + 1) * P], gate_sb[:, :],
                              start=True, stop=True)
                last.then_inc(p_logit, 1)

            def ranks(g):
                pe.wait_ge(a_es, g + 1)
                pe.wait_ge(d_chosen, g + 1)
                for u in range(G):
                    mm(M0[:, u * E:(u + 1) * E], upper[:, :], chosen[:, u, :], start=True, stop=(u == 0))
                    for b in range(u):
                        mm(M0[:, u * E:(u + 1) * E], ones_bf[:, :], chosen[:, b, :], start=False,
                           stop=(b == u - 1))
                for u in range(G):
                    last = mm(M0[:, G * E:(G + 1) * E], ones_bf[:, :], chosen[:, u, :], start=(u == 0),
                              stop=(u == G - 1))
                last.then_inc(p_rank, 1)

            def table(h):
                pe.wait_ge(d_tab, h + 1)
                for n, t in enumerate((cmp, cmp2)):
                    if n:
                        pe.wait_ge(d_tabe, 2 * h + 1)
                    for c in range(TC):
                        last = mm(M0[0:E, c * E:(c + 1) * E], t[:, c, :], ident[0:E, 0:E], start=True, stop=True)
                    last.then_inc(p_tab, 1)

            def slot(t, u, i2, p, groups_behind=2, new=True, nextp=True, one_back=True):
                g = 2 * i2 + p
                two_back = groups_behind > 0 or u > 1
                before_u, before_p = (u - 1) % G, p if u else 1 - p
                route = new and groups_behind > 0
                if u == 1 and nextp:
                    prep_tokens(g + 1)
                if u == 2 and route:
                    normed2_across(g - 1, 1 - p)
                if new:
                    if u == 0:
                        pe.wait_ge(a_q, g + 1)
                        pe.wait_ge(a_bd, g + 1)
                        pe.wait_ge(a_v, g + 1)
                    scores(t, u, p, 0)
                if two_back:
                    project(t - 2)
                if new:
                    scores(t, u, p, 1)
                if u == 1 and nextp:
                    pe.wait_ge(a_xnt, g + 2)
                if u == 2 and route:
                    pe.wait_ge(a_xn2t, g)
                if one_back:
                    for i in range(4):
                        probs_across(t - 1, i)
                if u == 0 and groups_behind > 1:
                    ranks(g - 2)
                if u == 1 and nextp:
                    prep_q(g + 1)
                if u == 2 and route:
                    if nextp:
                        pe.wait_ge(a_bd, g + 2)
                    else:
                        pe.wait_ge(d_slots, g - 1)
                    logits(g - 1, 1 - p)
                if one_back:
                    weighted_values(t - 1, before_u, before_p)
                if u == 1 and nextp:
                    prep_k(g + 1, 1 - p, i2 + p)
                if u == 2 and nextp:
                    if route:
                        pe.wait_ge(a_es, g)
                    prep_v(g + 1, 1 - p)

            def step(i2, p, groups_behind=2, last=False, half=False):
                for u in range(G):
                    slot(G * (2 * i2 + p) + u, u, i2, p, groups_behind=groups_behind, nextp=not last,
                         one_back=groups_behind > 0 or u > 0)
                if half:
                    pe.wait_ge(a_v, 2 * i2 + p + 2)
                    table(0)

            pe.wait_ge(s_const, 8)
            pe.wait_ge(s_init, 1)
            pe.wait_ge(s_vinit, 1)
            pe.wait_ge(s_w, 16 * 10)
            prep_tokens(0)
            prep_q(0)
            prep_k(0, 0, 0)
            prep_v(0, 0)
            step(0, 0, groups_behind=0)
            step(0, 1, groups_behind=1)
            with pe.Fori(1, HG // 2) as i2:
                step(i2, 0)
                step(i2, 1)
            step(HG // 2, 0)
            step(HG // 2, 1, half=True)
            with pe.Fori(HG // 2 + 1, NG // 2 - 1) as i2:
                step(i2, 0)
                step(i2, 1)
            step(NG // 2 - 1, 0)
            step(NG // 2 - 1, 1, last=True)
            slot(NT, 0, NG // 2, 0, new=False, nextp=False)
            slot(NT + 1, 1, NG // 2, 0, new=False, nextp=False, one_back=False)
            pe.wait_ge(d_slots, NG - 1)
            normed2_across(NG - 1, 1)
            logits(NG - 1, 1)
            ranks(NG - 1)
            table(1)

            def turn(j, r, round_):
                pe.wait_ge(s_rin[r], 16 * G * round_)
                for u in range(G):
                    last = nc.tensor.transpose(PX[:, u * P:(u + 1) * P], rin[r][:, u, 0:D], ident[:, :])
                last.then_inc(p_bx, 1)

            def gate_up(j):
                ex = read_four(mybir.EngineType.PE, tile_exp, j * G, E - 1)
                pe.wait_ge(a_bx, j + 1)
                wait(pe, d_bh, j)
                for u in range(G):
                    last = mm(banks[:, u // 2, (u % 2) * WGU:(u % 2 + 1) * WGU], b_xt[:, u * P:(u + 1) * P],
                              wgu[:, bass.ds(ex[u], 1), :], start=True, stop=True)
                last.then_inc(p_bgu, 1)

            def down(j):
                ex = read_four(mybir.EngineType.PE, tile_exp, j * G, E - 1)
                pe.wait_ge(a_bht, j + 1)
                wait(pe, d_by, j)
                for u in range(G):
                    last = mm(PY[:, u * D:(u + 1) * D], b_ht[0:I, u * P:(u + 1) * P],
                              wd[:, bass.ds(ex[u], 1), :], start=True, stop=True)
                last.then_inc(p_by, 1)

            def expert_steps(i, last_one=False):
                for q in range(STEPS):
                    j = STEPS * i + q
                    more = not (last_one and q == STEPS - 1)
                    if more:
                        turn(j + 1, (q + 1) % RING, 2 * i + ((q + 1) // RING + 1))
                    pe.wait_ge(d_bh, j + 1)
                    for u in range(G):
                        last = nc.tensor.transpose(PH[0:I, u * P:(u + 1) * P], b_h[:, u * I:(u + 1) * I],
                                                   ident[:, :])
                    last.then_inc(p_bht, 1)
                    if more:
                        gate_up(j + 1)
                    down(j)
                    if q in (2, 5):
                        a = (q - 2) // 3
                        if a == 0:
                            pe.wait_ge(s_shx, 16 * i + 16)
                        toks = sh_x[:, :]
                        mm(SHG[0:I, :], sg_w[:, a * I:(a + 1) * I], toks, start=True, stop=True)
                        mm(SHU[0:I, :], su_w[:, a * I:(a + 1) * I], toks, start=True, stop=True).then_inc(p_shgu, 1)
                    if q == 7:
                        pe.wait_ge(d_shh, 2 * i + 2)
                        for u in range(G):
                            for a in range(2):
                                last = mm(SHO[:, u * D:(u + 1) * D], sh_h[:, a, u * P:(u + 1) * P], sd_w[:, a, :],
                                          start=(a == 0), stop=(a == 1))
                        last.then_inc(p_sho, 1)

            pe.wait_ge(s_wexp, 16 * 6)
            pe.wait_ge(d_tabe, 4)
            turn(0, 0, 1)
            gate_up(0)
            expert_steps(0)
            with pe.Fori(1, NG - 1) as i:
                expert_steps(i)
            expert_steps(NG - 1, last_one=True)


_NAMES = ["x", "ctx_768", "wq", "bq", "wk", "bk", "wv", "bv", "wo", "bo", "gate_w", "gate_bias",
          "Wg", "Wu", "Wd", "Sg", "Su", "Sd"]


def kernel(**inputs):
    import numpy as _np
    import concourse.bacc as _bacc
    from concourse import mybir as _mybir
    from concourse.bass_utils import run_bass_kernel_spmd as _run

    a = {}
    for name in _NAMES:
        full = name if name in inputs else ("L0_xattn_" if "L0_xattn_" + name in inputs else "L0_ffn_") + name
        a[name] = _np.asarray(inputs[full])
    a["ctx_768"] = a["ctx_768"].transpose(2, 0, 1).reshape(DC, NT * SK)
    a["gate_w"] = a["gate_w"].T
    for name in ("Wg", "Wu"):
        a[name] = a[name].transpose(2, 0, 1)
    a["Wd"] = a["Wd"].transpose(2, 0, 1)
    for name in ("Sg", "Su", "Sd"):
        a[name] = a[name].T
    nc = _bacc.Bacc("TRN2", target_bir_lowering=False, num_devices=1)
    arrays, args = {}, []
    for name in _NAMES:
        arr = _np.ascontiguousarray(a[name])
        arrays[f"in_{name}"] = arr
        args.append(nc.dram_tensor(f"in_{name}", arr.shape, _mybir.dt.from_np(arr.dtype), kind="ExternalInput").ap())
    args.append(nc.dram_tensor("out_0", (NT, P, D), _mybir.dt.float32, kind="ExternalOutput").ap())
    moe_block(nc, *args)
    r = _run(nc, [arrays], core_ids=[0])
    return r.results[0]["out_0"]
```
